# Optimizing a Trainium2 kernel written in Bass

```python
import numpy as np
import jax
import jax.numpy as jnp

def _softmax(x, axis=-1):
    return jax.nn.softmax(x, axis=axis)

def _gelu(x):
    return jax.nn.gelu(x, approximate=True)

def _silu(x):
    return jax.nn.silu(x)

def _sigmoid(x):
    return jax.nn.sigmoid(x)

def _layernorm(x, axis=-1, eps=1e-05):
    m = jnp.mean(x, axis=axis, keepdims=True)
    v = jnp.var(x, axis=axis, keepdims=True)
    return (x - m) / jnp.sqrt(v + eps)

def _scatter_add(tgt, idx, src, axis=0):
    return tgt.at[idx].add(src)

def _segment_sum(src, seg, n):
    return jax.ops.segment_sum(src, seg, n)
kernel_name = 'mk_gnn_resnorm_d2_gnn_r16_10d177'

def setup_inputs(seed: int=0):
    np.random.seed(seed)
    _w = jnp.asarray

    def _rec_inputs():
        import jax
        import jax.numpy as jnp
        _gk = jax.random.key(seed)
        x = -0.000202 + 1 * jax.random.normal(jax.random.fold_in(_gk, 1), (6250, 128), jnp.float32)
        _s = jax.random.randint(jax.random.fold_in(_gk, 2), (100000,), 0, 6250, jnp.int32)
        _d = jax.random.randint(jax.random.fold_in(_gk, 3), (100000,), 0, 6250, jnp.int32)
        _loop = jnp.arange(6250, dtype=jnp.int32)
        src = jnp.concatenate([_s, _d, _loop])
        dst = jnp.concatenate([_d, _s, _loop])
        _o = jnp.argsort(dst, stable=True)
        src = src[_o]
        dst = dst[_o]
        edge_type_4 = jax.random.randint(jax.random.fold_in(_gk, 12), (206250,), 0, 4, jnp.int32)
        edge_weight = jax.random.uniform(jax.random.fold_in(_gk, 13), (206250,), jnp.float32, 0.0, 0.999999)
        return (x, src, dst, edge_type_4, edge_weight)
    x, src, dst, edge_type_4, edge_weight = _rec_inputs()

    def _L0_gnn_setup():
        import jax, jax.numpy as jnp
        import numpy as np
        N_TYPES = 4
        NEG_SLOPE = 0.01

        def _conv(x, row, col, edge_type, edge_weight, W, b):
            N = x.shape[0]
            deg = jax.ops.segment_sum(jnp.ones(col.shape[0], dtype=x.dtype), col, num_segments=N)
            deg_inv_sqrt = jnp.where(deg > 0, deg ** (-0.5), jnp.zeros((), x.dtype))
            norm = deg_inv_sqrt[row] * deg_inv_sqrt[col] * edge_weight
            xw = jnp.einsum('ni,tio->tno', x, W)
            x_j = xw[edge_type, col] * norm[:, None]
            out = jax.ops.segment_sum(x_j, row, num_segments=N) + b
            return jax.nn.leaky_relu(out, negative_slope=NEG_SLOPE)
        key = jax.random.key(seed)
        ks = jax.random.split(key, 10)
        N, d, E = (3125, 128, 625000)
        x = jax.random.normal(ks[0], (N, d), dtype=jnp.float32)
        edge_index = jax.random.randint(ks[1], (2, E), 0, N, dtype=jnp.int64 if jax.config.jax_enable_x64 else jnp.int32)
        edge_type = jax.random.randint(ks[2], (E,), 0, N_TYPES)
        edge_attr = jax.random.uniform(ks[3], (E,), dtype=jnp.float32)
        bound = float(np.sqrt(6.0 / (d + d)))
        W1 = jax.random.uniform(ks[4], (N_TYPES, d, d), minval=-bound, maxval=bound, dtype=jnp.float32)
        W2 = jax.random.uniform(ks[5], (N_TYPES, d, d), minval=-bound, maxval=bound, dtype=jnp.float32)
        W3 = jax.random.uniform(ks[6], (N_TYPES, d, d), minval=-bound, maxval=bound, dtype=jnp.float32)
        b1 = jnp.zeros((d,), jnp.float32)
        b2 = jnp.zeros((d,), jnp.float32)
        b3 = jnp.zeros((d,), jnp.float32)
        return {'x': x, 'edge_index': edge_index, 'edge_type': edge_type, 'edge_attr': edge_attr, 'W1': W1, 'b1': b1, 'W2': W2, 'b2': b2, 'W3': W3, 'b3': b3}
    _L0_gnn_all = _L0_gnn_setup()
    _L0_gnn_in = {k: v for k, v in _L0_gnn_all.items() if k in ('W1', 'b1', 'W2', 'b2', 'W3', 'b3')}
    del _L0_gnn_all

    def _L1_gnn_setup():
        import jax, jax.numpy as jnp
        import numpy as np
        N_NODES = 3125
        N_EDGES = 100000
        IN_CH = 128
        OUT_CH = 64
        HEADS = 2
        NEG_SLOPE = 0.2
        key = jax.random.key(seed)
        ks = jax.random.split(key, 8)
        x = jax.random.normal(ks[0], (N_NODES, IN_CH), dtype=jnp.float32)
        edge_index = jax.random.randint(ks[1], (2, N_EDGES), 0, N_NODES, dtype=jnp.int64)
        edge_weight = jax.random.uniform(ks[2], (N_EDGES,), dtype=jnp.float32)
        W = jax.random.normal(ks[3], (IN_CH, HEADS * OUT_CH), dtype=jnp.float32) * (1.0 / np.sqrt(IN_CH))
        att_src = jax.random.normal(ks[4], (HEADS, OUT_CH), dtype=jnp.float32) * (1.0 / np.sqrt(OUT_CH))
        att_dst = jax.random.normal(ks[5], (HEADS, OUT_CH), dtype=jnp.float32) * (1.0 / np.sqrt(OUT_CH))
        bias = jnp.zeros((HEADS * OUT_CH,), dtype=jnp.float32)
        return {'x': x, 'edge_index': edge_index, 'edge_weight': edge_weight, 'W': W, 'att_src': att_src, 'att_dst': att_dst, 'bias': bias}
    _L1_gnn_all = _L1_gnn_setup()
    _L1_gnn_in = {k: v for k, v in _L1_gnn_all.items() if k in ('W', 'att_src', 'att_dst', 'bias')}
    del _L1_gnn_all
    return {'x': x, 'src': src, 'dst': dst, 'edge_type_4': edge_type_4, 'edge_weight': edge_weight, 'L0_gnn_W1': _L0_gnn_in['W1'], 'L0_gnn_b1': _L0_gnn_in['b1'], 'L0_gnn_W2': _L0_gnn_in['W2'], 'L0_gnn_b2': _L0_gnn_in['b2'], 'L0_gnn_W3': _L0_gnn_in['W3'], 'L0_gnn_b3': _L0_gnn_in['b3'], 'L1_gnn_W': _L1_gnn_in['W'], 'L1_gnn_att_src': _L1_gnn_in['att_src'], 'L1_gnn_att_dst': _L1_gnn_in['att_dst'], 'L1_gnn_bias': _L1_gnn_in['bias']}

def reference(x, src, dst, edge_type_4, edge_weight, L0_gnn_W1, L0_gnn_b1, L0_gnn_W2, L0_gnn_b2, L0_gnn_W3, L0_gnn_b3, L1_gnn_W, L1_gnn_att_src, L1_gnn_att_dst, L1_gnn_bias):
    import jax
    import jax.numpy as jnp

    def _L0_gnn_ref(x, edge_index, edge_type, edge_attr, W1, b1, W2, b2, W3, b3):
        import jax, jax.numpy as jnp
        import numpy as np
        N_TYPES = 4
        NEG_SLOPE = 0.01

        def _conv(x, row, col, edge_type, edge_weight, W, b):
            N = x.shape[0]
            deg = jax.ops.segment_sum(jnp.ones(col.shape[0], dtype=x.dtype), col, num_segments=N)
            deg_inv_sqrt = jnp.where(deg > 0, deg ** (-0.5), jnp.zeros((), x.dtype))
            norm = deg_inv_sqrt[row] * deg_inv_sqrt[col] * edge_weight
            xw = jnp.einsum('ni,tio->tno', x, W)
            x_j = xw[edge_type, col] * norm[:, None]
            out = jax.ops.segment_sum(x_j, row, num_segments=N) + b
            return jax.nn.leaky_relu(out, negative_slope=NEG_SLOPE)
        row, col = (edge_index[0], edge_index[1])
        z1 = _conv(x, row, col, edge_type, edge_attr, W1, b1)
        z2 = _conv(z1, row, col, edge_type, edge_attr, W2, b2)
        z3 = _conv(z2, row, col, edge_type, edge_attr, W3, b3)
        return (x + z1 + z2 + z3) / 4

    def _L1_gnn_ref(x, edge_index, edge_weight, W, att_src, att_dst, bias):
        import jax, jax.numpy as jnp
        import numpy as np
        N_NODES = 3125
        N_EDGES = 100000
        IN_CH = 128
        OUT_CH = 64
        HEADS = 2
        NEG_SLOPE = 0.2
        x_masked = x * (x != 0.0).astype(x.dtype)
        n = x.shape[0]
        xp = (x_masked @ W).reshape(n, HEADS, OUT_CH)
        loops = jnp.arange(n, dtype=edge_index.dtype)
        src = jnp.concatenate([edge_index[0], loops])
        dst = jnp.concatenate([edge_index[1], loops])
        a_src = jnp.einsum('nhc,hc->nh', xp, att_src)
        a_dst = jnp.einsum('nhc,hc->nh', xp, att_dst)
        alpha = jax.nn.leaky_relu(a_src[src] + a_dst[dst], NEG_SLOPE)
        m = jax.ops.segment_max(alpha, dst, num_segments=n)
        e = jnp.exp(alpha - m[dst])
        s = jax.ops.segment_sum(e, dst, num_segments=n)
        alpha = e / (s[dst] + 1e-16)
        msg = alpha[:, :, None] * xp[src]
        out = jax.ops.segment_sum(msg, dst, num_segments=n)
        return out.reshape(n, HEADS * OUT_CH) + bias
    edge_index = jnp.stack([src, dst])
    x = _layernorm(x + _L0_gnn_ref(x, edge_index, edge_type_4, edge_weight, L0_gnn_W1, L0_gnn_b1, L0_gnn_W2, L0_gnn_b2, L0_gnn_W3, L0_gnn_b3), axis=-1)
    x = _layernorm(x + _L1_gnn_ref(x, edge_index, edge_weight, L1_gnn_W, L1_gnn_att_src, L1_gnn_att_dst, L1_gnn_bias), axis=-1)
    return x

_drawn_inputs = setup_inputs


def setup_inputs(seed=0):
    import zlib

    import numpy as np

    out = dict(_drawn_inputs(seed))
    spreads = {'L0_gnn_b1': (0.0, 0.486),
     'L0_gnn_b2': (0.0, 2.0),
     'L0_gnn_b3': (0.0, 2.0),
     'L1_gnn_bias': (0.0, 0.1)}
    factors = {'edge_weight': 8.0,
     'L0_gnn_W1': 4.376,
     'L0_gnn_W2': 8.0,
     'L0_gnn_W3': 8.0,
     'L1_gnn_att_src': 3.029,
     'L1_gnn_att_dst': 4.972}
    for name, (base, spread) in spreads.items():
        noise = np.random.default_rng([zlib.crc32(name.encode()), seed]).standard_normal(out[name].shape)
        drawn = base * np.exp(spread * noise) if base else spread * noise
        out[name] = jnp.asarray(drawn.astype(out[name].dtype))
    for name, factor in factors.items():
        out[name] = (out[name] * factor).astype(out[name].dtype)
    return out
```

```python
from contextlib import ExitStack

import concourse.bass as bass
from concourse import mybir

F32, BF16 = mybir.dt.float32, mybir.dt.bfloat16
I32, U32, U8 = mybir.dt.int32, mybir.dt.uint32, mybir.dt.uint8
ALU = mybir.AluOpType
ACT = mybir.ActivationFunctionType
AX = mybir.AxisListType

P = 128
N_NODES, D, N_EDGES, N_TYPES, HEADS = 6250, 128, 206250, 4, 2
HC = D // HEADS
NB = -(-N_NODES // P)
FULL, REST = N_NODES // P, N_NODES % P
PAD_NODE = NB * P
NBINS = NB + 1
COLS = -(-N_EDGES // P)
LAST_COLS = N_EDGES - (P - 1) * COLS
SCATTER = 31
HIST = 13
BIG = 2.0 ** 100
NO_NODE = -1.0


class Plan:

    def __init__(self, tiles, part, ring):
        self.tiles, self.part, self.ring = tiles, part, ring
        per = tiles * P
        most = (N_EDGES + NB * (per - 1)) // per
        self.steps = -(-most // part)
        self.groups = self.steps * part
        self.step_tiles = tiles * part
        self.slots = max(self.groups * tiles, (most + 1) * tiles)
        self.shift = per.bit_length() - 1


GCN = Plan(tiles=2, part=5, ring=3)
GAT = Plan(tiles=4, part=1, ring=5)
ROW = HEADS * (HC + 1) + HEADS
STATE = 3 * HEADS


class Step:

    def __init__(self, plan, base, i=None):
        self.plan, self.base, self.i = plan, base, i

    def live(self, lag):
        return self.i is not None or 0 <= self.base + lag < self.plan.steps

    def slot(self, lag):
        return (self.base + lag) % self.plan.ring

    def at(self, lag, times=1, plus=0):
        c = (self.base + lag) * times + plus
        return c if self.i is None else self.i * (self.plan.ring * times) + c

    def landed(self, lag, earlier=0):
        c = 16 * ((self.base + lag) // self.plan.ring + 1 + earlier)
        return c if self.i is None else self.i * 16 + c


def run_steps(eng, plan, behind, ahead, body):
    whole = (plan.steps - ahead - behind) // plan.ring
    start, end = behind, behind + whole * plan.ring
    for q in range(-ahead, start):
        body(Step(plan, q))
    with eng.Fori(0, whole) as i:
        for j in range(plan.ring):
            body(Step(plan, start + j, i))
    for q in range(end, plan.steps + behind):
        body(Step(plan, q))


def wait_apart(eng, sem, value, count):
    eng.wait_ge(sem, value)
    eng.sem_inc(count, 1)


class Chain:

    def __init__(self, eng, sem):
        self.eng, self.sem, self.n = eng, sem, 0

    def __call__(self, ins):
        ins.then_inc(self.sem, 1)
        self.n += 1
        self.eng.wait_ge(self.sem, self.n)


def gnn_kernel(nc, x, src, dst, etype, weight, w1, b1, w2, b2, w3, b3, w_gat, att_src, att_dst,
               bias_gat, out):
    ctx = ExitStack()
    with ctx:
        def sb(name, shape, dt=F32, scope=ctx):
            return scope.enter_context(nc.sbuf_tensor(name, shape, dt))

        def sem(name):
            return ctx.enter_context(nc.semaphore(name))

        gcn_slots = nc.dram_tensor("gcn_slots", [P * GCN.slots, 3], F32).ap()
        gat_slots = nc.dram_tensor("gat_slots", [P * GAT.slots, 2], F32).ap()
        gcn_table = nc.dram_tensor("gcn_table", [NB * P * N_TYPES, D], F32).ap()
        gat_table = nc.dram_tensor("gat_table", [NB * P, ROW], F32).ap()

        iota = sb("iota", [P, P])
        iota_n = sb("iota_n", [P, GCN.groups])
        ident = sb("ident", [P, P])
        before = sb("before", [P, P])
        ones = sb("ones", [P, P])
        zeros = sb("zeros", [P, COLS], BF16)
        w_all = sb("w_all", [P, 3, N_TYPES * D])
        w_att = sb("w_att", [P, D])
        bias = sb("bias", [P, 4, D])
        att = sb("att", [P, 2, D])
        inv_deg = sb("inv_deg", [P, NB])
        deg_mask = sb("deg_mask", [P, NB])
        gcn_block = sb("gcn_block", [1, GCN.groups], I32)
        gat_block = sb("gat_block", [1, GCN.groups], I32)
        gcn_rec = sb("gcn_rec", [P, GCN.slots, 3])
        gat_rec = sb("gat_rec", [P, GAT.slots, 2])
        xs = sb("xs", [P, NB, D])
        stats = sb("stats", [P, NB, 6])
        mv = sb("mv", [P, NB, 2])
        nodeT = sb("nodeT", [P, 2, P])
        rows = sb("rows", [P, 4, N_TYPES * D])

        sort = ExitStack()
        src_i = sb("src_i", [P, COLS], I32, sort)
        dst_i = sb("dst_i", [P, COLS], I32, sort)
        type_i = sb("type_i", [P, COLS], I32, sort)
        tmp_i = sb("tmp_i", [P, COLS], I32, sort)
        w_f = sb("w_f", [P, COLS], F32, sort)
        block_of = [sb(f"block_of{s}", [P, COLS], F32, sort) for s in range(2)]
        dst_lo = sb("dst_lo", [P, COLS], F32, sort)
        mask = sb("mask", [P, COLS], U8, sort)
        rank = sb("rank", [P, COLS], F32, sort)
        place = w_f
        place_u = [sb("place_u0", [P, COLS], U32, sort)[:, :],
                   src_i[:, :].bitcast(U32)]
        rec_src = [sb("gcn_src", [P, COLS, 3], F32, sort), sb("gat_src", [P, COLS, 2], F32, sort)]
        at_stage = [[sb(f"at_stage{s}{h}", [P, SCATTER], U32, sort) for h in range(2)] for s in range(2)]
        rec_stage = [[sb(f"rec_stage{s}{h}", [P, SCATTER * (3 - s)], F32, sort) for h in range(2)]
                     for s in range(2)]
        lo_hot = sb("lo_hot", [P, 2, HIST, P], BF16, sort)
        hi_hot = sb("hi_hot", [P, 2, HIST, NB], BF16, sort)
        bins = sb("bins", [P, 8, NBINS], F32, sort)
        bins_i = sb("bins_i", [P, NBINS], I32, sort)
        start_col = sb("start_col", [NB, 1], F32, sort)
        passed = sb("passed", [NB, GCN.groups], F32, sort)
        sort.close()

        acc = sb("acc", [P, NB, HEADS * (HC + 1)])
        z = sb("z", [P, NB, D])
        gcn_scope = ExitStack()
        g_idx = sb("g_idx", [P, GCN.ring, GCN.step_tiles], U32, gcn_scope)
        g_lw = sb("g_lw", [P, GCN.ring, GCN.step_tiles, 2], F32, gcn_scope)
        g_rows = sb("g_rows", [P, GCN.ring, GCN.step_tiles, D], F32, gcn_scope)
        g_hot = sb("g_hot", [P, GCN.ring, GCN.step_tiles, P], F32, gcn_scope)
        gcn_scope.close()
        T, R = GAT.tiles, GAT.ring
        a_idx = sb("a_idx", [P, R, T], U32)
        a_lo = sb("a_lo", [P, R, T])
        a_rows = sb("a_rows", [P, R, T, ROW])
        a_hide = sb("a_hide", [P, R, T, P])
        a_hot = sb("a_hot", [P, R, T, P])
        a_cand = sb("a_cand", [P, HEADS, T, P])
        a_hotT = sb("a_hotT", [P, R, T, P])
        a_msg = sb("a_msg", [P, R, T, HEADS * (HC + 1)])
        a_max = sb("a_max", [P, R, HEADS])
        a_sum = sb("a_sum", [P, R, HEADS])
        a_node = sb("a_node", [P, R, 2 * HEADS])
        a_drop = sb("a_drop", [P, R, HEADS])
        a_scale = sb("a_scale", [P, R, HEADS])
        a_z = sb("a_z", [P, R, T, HEADS])
        a_l = sb("a_l", [P, R, T, HEADS])
        a_e = sb("a_e", [P, R, T, HEADS])
        a_p = sb("a_p", [P, R, T, HEADS])
        state = sb("state", [P, NB, 3, HEADS])
        att_tmp = sb("att_tmp", [P, 2, 2, D])

        bank = [ctx.enter_context(nc.psum_tensor(f"bank{k}", [P, 512], F32)) for k in range(6)]
        wide = ctx.enter_context(nc.psum_tensor("wide", [P, HEADS, T, P], F32))

        s_const, s_fill, s_chain = sem("s_const"), sem("s_fill"), sem("s_chain")
        s_in = {n: sem(f"s_in_{n}") for n in ("src", "dst", "type", "weight", "x", "w", "bias", "att")}
        s_seed, s_recs, s_recs_load = sem("s_seed"), sem("s_recs"), sem("s_recs_load")
        s_pre = sem("s_pre")
        s_pfx = sem("s_pfx")
        s_scol, s_scol2 = sem("s_scol"), sem("s_scol2")
        s_pass, s_pass2 = sem("s_pass"), sem("s_pass2")
        s_place = sem("s_place")
        s_stg = [[sem(f"s_stg{s}{h}") for h in range(2)] for s in range(2)]
        s_sct = [[sem(f"s_sct{s}{h}") for h in range(2)] for s in range(2)]
        s_hot, s_cnt = sem("s_hot"), sem("s_cnt")
        s_sqrt = sem("s_sqrt")
        s_sorted = sem("s_sorted")
        s_g = [sem(f"s_g{k}") for k in range(GCN.ring * GCN.step_tiles)]
        s_stage, s_ghot, s_gpe, s_gadd = ([sem(f"{n}{l}") for l in range(3)]
                                          for n in ("s_stage", "s_ghot", "s_gpe", "s_gadd"))
        s_z = [sem(f"s_z{l}") for l in range(4)]
        s_tT = [sem(f"s_tT{l}") for l in range(4)]
        s_tc = [sem(f"s_tc{l}") for l in range(4)]
        s_tm = [sem(f"s_tm{l}") for l in range(4)]
        s_tr = [sem(f"s_tr{l}") for l in range(4)]
        s_tw = [sem(f"s_tw{k}") for k in range(4)]
        s_ln, s_ln2 = sem("s_ln"), sem("s_ln2")
        s_xr = sem("s_xr")
        sa = {n: sem(f"sa_{n}") for n in ("stage", "hide", "cand", "T", "hotT", "m", "scale", "node",
                                          "e", "p", "msg", "pv", "add")}
        s_ag = [sem(f"s_ag{k}") for k in range(R * T)]
        s_apart = [sem("s_apart_pool"), sem("s_apart_dve")]
        s_fin, s_out = sem("s_fin"), sem("s_out")

        def spread(ap, shape):
            return ap.to_broadcast(shape)

        block = ctx.enter_context(nc.Block())
        TABLE_TURNS = [NB] * 4

        def tw_before(layer, k):
            return layer * len(range(k, NB, 4))

        @block.sync
        def _(sp):
            def load_edges(name, dram, tile):
                flat = dram.rearrange("(o n) -> o n", o=1)
                body = flat[0:1, 0:(P - 1) * COLS].rearrange("o (p c) -> (o p) c", p=P - 1)
                sp.dma_start(tile[0:P - 1, :], body).then_inc(s_in[name], 16)
                sp.dma_start(tile[P - 1:P, 0:LAST_COLS], flat[0:1, (P - 1) * COLS:]).then_inc(s_in[name], 16)

            sp.wait_ge(s_fill, 4)
            load_edges("src", src, src_i)
            load_edges("dst", dst, dst_i)
            load_edges("type", etype, type_i)
            load_edges("weight", weight, w_f)
            sp.wait_ge(s_fill, 5)
            sp.dma_start(xs[:, 0:FULL, :],
                         x[0:FULL * P, :].rearrange("(b p) f -> p b f", p=P)).then_inc(s_in["x"], 16)
            sp.dma_start(xs[0:REST, FULL, :], x[FULL * P:, :]).then_inc(s_in["x"], 16)
            for l, w in enumerate((w1, w2, w3)):
                sp.dma_start(w_all[:, l, :].rearrange("i (t o) -> i t o", t=N_TYPES),
                             w.rearrange("t i o -> i t o")).then_inc(s_in["w"], 16)
            sp.dma_start(w_att[:, :], w_gat).then_inc(s_in["w"], 16)
            for l, b in enumerate((b1, b2, b3, bias_gat)):
                sp.dma_start(bias[:, l, :], b.partition_broadcast(P)).then_inc(s_in["bias"], 16)
            for l, a in enumerate((att_src, att_dst)):
                sp.dma_start(att[:, l, :], a.rearrange("h c -> (h c)").partition_broadcast(P)
                             ).then_inc(s_in["att"], 16)
            sp.wait_ge(s_fill, 9)
            sp.dma_start(gcn_slots.rearrange("(p t) k -> p (t k)", p=P),
                         gcn_rec[:, :, :].rearrange("p t k -> p (t k)")).then_inc(s_seed, 16)
            sp.dma_start(gat_slots.rearrange("(p t) k -> p (t k)", p=P),
                         gat_rec[:, :, :].rearrange("p t k -> p (t k)")).then_inc(s_seed, 16)

            def write_table(layer, table):
                for b in range(NB):
                    k = b % 4
                    sp.wait_ge(s_tr[layer], b + 1)
                    width = table.shape[1]
                    sp.dma_start(table[b * P:(b + 1) * P, :],
                                 rows[:, k, 0:width]).then_inc(s_tw[k], 16)

            gcn_wide = gcn_table.rearrange("(n t) f -> n (t f)", t=N_TYPES)
            write_table(0, gcn_wide)
            for s, (dram, tile) in enumerate(((gcn_slots, gcn_rec), (gat_slots, gat_rec))):
                for h in range(2):
                    sp.wait_ge(s_sct[s][h], 16 * SCATTER * (COLS // (2 * SCATTER)))
                sp.dma_start(tile[:, :, :].rearrange("p t k -> p (t k)"),
                             dram.rearrange("(p t) k -> p (t k)", p=P)).then_inc(s_recs_load, 16)
            write_table(1, gcn_wide)
            write_table(2, gcn_wide)
            sp.wait_ge(s_xr, 1)
            sp.dma_start(z[:, 0:FULL, :],
                         x[0:FULL * P, :].rearrange("(b p) f -> p b f", p=P)).then_inc(s_in["x"], 16)
            sp.dma_start(z[0:REST, FULL, :], x[FULL * P:, :]).then_inc(s_in["x"], 16)
            write_table(3, gat_table)
            sp.wait_ge(s_fin, 1)
            sp.dma_start(out[0:FULL * P, :].rearrange("(b p) f -> p b f", p=P),
                         xs[:, 0:FULL, :]).then_inc(s_out, 16)
            sp.dma_start(out[FULL * P:, :], xs[0:REST, FULL, :]).then_inc(s_out, 16)
            sp.wait_ge(s_out, 32)

        @block.gpsimd
        def _(pool):
            nc.gpsimd.iota(iota[:, :], [[1, P]], base=0, channel_multiplier=0,
                           allow_small_or_imprecise_dtypes=True)
            nc.gpsimd.iota(iota_n[:, :], [[1, GCN.groups]], base=0, channel_multiplier=0,
                           allow_small_or_imprecise_dtypes=True)
            nc.gpsimd.memset(ones[:, :], 1.0).then_inc(s_const, 1)
            pool.wait_ge(s_const, 1)
            nc.gpsimd.affine_select(out=ident[:, :], in_=ones[:, :], compare_op=ALU.is_equal, fill=0.0,
                                    base=0, pattern=[[1, P]], channel_multiplier=-1)
            nc.gpsimd.affine_select(out=before[:, :], in_=ones[:, :], compare_op=ALU.is_gt, fill=0.0,
                                    base=0, pattern=[[1, P]], channel_multiplier=-1).then_inc(s_const, 1)
            pool.wait_ge(s_seed, 32)
            for s, dram in enumerate((gcn_slots, gat_slots)):
                k = 3 - s
                with pool.Fori(0, COLS // (2 * SCATTER)) as i:
                    for h in range(2):
                        wait_apart(pool, s_stg[s][h], i * 2 + 2, s_apart[0])
                        for c in range(SCATTER):
                            pool.indirect_dma_start(
                                out=dram, out_offset=bass.IndirectOffsetOnAxis(
                                    ap=at_stage[s][h][:, c:c + 1], axis=0),
                                in_=rec_stage[s][h][:, c * k:(c + 1) * k], in_offset=None,
                            ).then_inc(s_sct[s][h], 16)

            def gather_gcn(layer):
                for k in range(4):
                    pool.wait_ge(s_tw[k], 16 * tw_before(layer + 1, k))

                def body(q):
                    wait_apart(pool, s_stage[layer], q.at(0, 2, 2), s_apart[0])
                    for t in range(GCN.step_tiles):
                        pool.indirect_dma_start(
                            out=g_rows[:, q.slot(0), t, :], out_offset=None, in_=gcn_table,
                            in_offset=bass.IndirectOffsetOnAxis(
                                ap=g_idx[:, q.slot(0), t:t + 1], axis=0),
                        ).then_inc(s_g[q.slot(0) * GCN.step_tiles + t], 16)
                run_steps(pool, GCN, 0, 0, body)

            for layer in range(3):
                gather_gcn(layer)

            for k in range(4):
                pool.wait_ge(s_tw[k], 16 * tw_before(4, k))

            def body(q):
                wait_apart(pool, sa["stage"], q.at(0, 1, 1), s_apart[0])
                for t in range(T):
                    pool.indirect_dma_start(
                        out=a_rows[:, q.slot(0), t, :], out_offset=None, in_=gat_table,
                        in_offset=bass.IndirectOffsetOnAxis(ap=a_idx[:, q.slot(0), t:t + 1], axis=0),
                    ).then_inc(s_ag[q.slot(0) * T + t], 16)
            run_steps(pool, GAT, 0, 0, body)

        @block.scalar
        def _(act):
            for s in range(2):
                k = 3 - s
                act.wait_ge(s_place, s + 1)

                def stage(i, h):
                    col = i * (2 * SCATTER) + h * SCATTER
                    nc.scalar.copy(at_stage[s][h][:, :], place_u[s][:, bass.ds(col, SCATTER)]
                                   ).then_inc(s_stg[s][h], 1)
                    nc.scalar.copy(rec_stage[s][h][:, :].rearrange("p (c k) -> p c k", k=k),
                                   rec_src[s][:, bass.ds(col, SCATTER), :]).then_inc(s_stg[s][h], 1)
                for h in range(2):
                    stage(0, h)
                turns = COLS // (2 * SCATTER)
                for first, end in ((1, turns // 2), (turns // 2, turns)):
                    with act.Fori(first, end) as i:
                        for h in range(2):
                            act.wait_ge(s_sct[s][h], i * (16 * SCATTER))
                            stage(i, h)
                    if s == 0 and first == 1:
                        act.wait_ge(s_sqrt, 1)
                        nc.scalar.sqrt(inv_deg[:, :], inv_deg[:, :]).then_inc(s_sqrt, 1)

            def table(layer):
                for b in range(NB):
                    act.wait_ge(s_tT[layer], b + 1)
                    nc.scalar.copy(nodeT[:, b % 2, :], bank[4 + b % 2][:, 0:P]
                                   ).then_inc(s_tc[layer], 1)
                    if b >= 1:
                        row(layer, b - 1)
                row(layer, NB - 1)

            def row(layer, b):
                act.wait_ge(s_tm[layer], b + 1)
                if b >= 4 or layer:
                    act.wait_ge(s_tw[b % 4], 16 * (tw_before(layer, b % 4) + b // 4))
                nc.scalar.activation(rows[:, b % 4, :], bank[2 + b % 2][:, :], ACT.Copy,
                                     scale=inv_deg[:, b:b + 1]).then_inc(s_tr[layer], 1)
            table(1)
            table(2)

            def ln_sqrt(n):
                act.wait_ge(s_ln, n)
                nc.scalar.sqrt(mv[:, :, 1], mv[:, :, 1]).then_inc(s_ln2, 1)

            ln_sqrt(1)
            for b in range(NB):
                act.wait_ge(s_tT[3], b + 1)
                nc.scalar.copy(nodeT[:, b % 2, :], bank[4 + b % 2][:, 0:P]
                               ).then_inc(s_tc[3], 1)

            def body(q):
                if q.live(1):
                    act.wait_ge(sa["m"], q.at(1, 6, 1))
                    nc.scalar.activation(a_hotT[:, q.slot(1), :, :], wide[:, 0, :, :], ACT.Identity,
                                         bias=1.0, scale=1.0 / BIG).then_inc(sa["hotT"], 1)
                if q.live(2):
                    act.wait_ge(sa["hide"], q.at(2, 1, 1))
                    nc.scalar.activation(a_hot[:, q.slot(2), :, :], a_hide[:, q.slot(2), :, :], ACT.Identity,
                                         bias=1.0, scale=1.0 / BIG)
                    for t in range(T):
                        act.wait_ge(s_ag[q.slot(2) * T + t], q.landed(2))
                        for h in range(HEADS):
                            last = nc.scalar.activation(
                                a_cand[:, h, t, :], a_hide[:, q.slot(2), t, :], ACT.Identity,
                                bias=a_rows[:, q.slot(2), t, ROW - HEADS + h:ROW - HEADS + h + 1])
                    last.then_inc(sa["cand"], 1)
                if q.live(1):
                    act.wait_ge(sa["m"], q.at(1, 6, 6))
                    nc.scalar.activation(a_scale[:, q.slot(1), :], a_drop[:, q.slot(1), :], ACT.Exp
                                         ).then_inc(sa["scale"], 1)
                if q.live(0):
                    act.wait_ge(sa["e"], q.at(0, 3, 3))
                    nc.scalar.activation(a_p[:, q.slot(0), :, :], a_e[:, q.slot(0), :, :], ACT.Exp
                                         ).then_inc(sa["p"], 1)

            run_steps(act, GAT, 2, 3, body)
            ln_sqrt(2)

        @block.tensor
        def _(pe):
            pe.wait_ge(s_const, 2)

            def ranks(s):
                pe.wait_ge(s_pre, s + 1)
                nc.tensor.matmul(bank[1][:, 0:NBINS], before[:, :], bins[:, 0, :], start=True, stop=True)
                nc.tensor.matmul(bank[1][:, 64:64 + NBINS], ones[:, :], bins[:, 0, :],
                                 start=True, stop=True).then_inc(s_pfx, 1)
                pe.wait_ge(s_scol, s + 1)
                nc.tensor.matmul(bank[0][0:NB, 500:501], bins[0:1, 4, 0:NB], ones[0:1, 0:1],
                                 start=True, stop=True).then_inc(s_scol2, 1)
                pe.wait_ge(s_pass, s + 1)
                half = GCN.groups // 2
                nc.tensor.matmul(bank[0][0:1, 0:half + 1], ones[0:NB, 0:1], passed[:, 0:half + 1],
                                 start=True, stop=True)
                nc.tensor.matmul(bank[5][0:1, 0:GCN.groups - half - 1], ones[0:NB, 0:1],
                                 passed[:, half + 1:], start=True, stop=True).then_inc(s_pass2, 1)

            ranks(0)
            pe.wait_ge(s_hot, 1)
            nc.tensor.matmul(bank[1][:, 256:256 + NB], lo_hot[:, 0, 0, :], zeros[:, 0:NB],
                             start=True, stop=False).then_inc(s_cnt, 1)
            with pe.Fori(0, COLS // (2 * HIST)) as i:
                for h in range(2):
                    pe.wait_ge(s_hot, i * 2 + h + 1)
                    for c in range(HIST):
                        last = nc.tensor.matmul(bank[1][:, 256:256 + NB], lo_hot[:, h, c, :],
                                                hi_hot[:, h, c, :], start=False, stop=False,
)
                    last.then_inc(s_cnt, 1)
            nc.tensor.matmul(bank[1][:, 256:256 + NB], lo_hot[:, 0, 0, :], zeros[:, 0:NB],
                             start=False, stop=True).then_inc(s_cnt, 1)

            def table(layer, node, w, evicted):
                def product(b):
                    pe.wait_ge(s_tc[layer], b + 1)
                    if b >= 2:
                        pe.wait_ge(s_tr[layer], b - 1)
                    nc.tensor.matmul(bank[2 + b % 2][:, 0:w.shape[1]], nodeT[:, b % 2, :], w,
                                     start=True, stop=True).then_inc(s_tm[layer], 1)
                for b in range(NB):
                    pe.wait_ge(s_z[layer], b + 1 if layer else 1)
                    if b >= 2:
                        pe.wait_ge(s_tc[layer], b - 1)
                    nc.tensor.transpose(bank[4 + b % 2][:, 0:P], node[:, b, :], ident[:, :]
                                        ).then_inc(s_tT[layer], 1)
                    if b >= 1:
                        product(b - 1)
                product(NB - 1)

            pe.wait_ge(s_in["x"], 32)
            pe.wait_ge(s_in["w"], 64)
            table(0, xs, w_all[:, 0, :], None)
            ranks(1)

            def sum_gcn(layer):
                def body(q):
                    j = q.slot(0)
                    pe.wait_ge(s_ghot[layer], q.at(0, 1, 1))
                    pe.wait_ge(s_gadd[layer], q.at(0, GCN.part, 1))
                    for g in range(GCN.part):
                        for t in range(GCN.tiles):
                            k = g * GCN.tiles + t
                            pe.wait_ge(s_g[j * GCN.step_tiles + k],
                                       q.landed(0, layer * len(range(j, GCN.steps, GCN.ring))))
                            last = nc.tensor.matmul(bank[g][:, 0:D], g_hot[:, j, k, :], g_rows[:, j, k, :],
                                                    start=(t == 0), stop=(t == GCN.tiles - 1))
                        last.then_inc(s_gpe[layer], 1)
                run_steps(pe, GCN, 0, 0, body)

            sum_gcn(0)
            table(1, z, w_all[:, 1, :], None)
            sum_gcn(1)
            table(2, z, w_all[:, 2, :], None)
            sum_gcn(2)
            table(3, z, w_att[:, :], None)

            def body(q):
                if q.live(1):
                    pe.wait_ge(sa["m"], q.at(1, 6, 6))
                    pe.wait_ge(sa["hotT"], q.at(1, 1, 1))
                    if q.live(0):
                        pe.wait_ge(sa["e"], q.at(0, 3, 3))
                    j = q.slot(1)
                    for t in range(T):
                        last = nc.tensor.matmul(bank[5][:, (j * T + t) * 4:(j * T + t + 1) * 4],
                                                a_hotT[:, j, t, :], a_node[:, j, :], start=True, stop=True)
                    last.then_inc(sa["node"], 1)
                if q.live(2):
                    pe.wait_ge(sa["cand"], q.at(2, 1, 1))
                    for h in range(HEADS):
                        for t in range(T):
                            last = nc.tensor.transpose(wide[:, h, t, :], a_cand[:, h, t, :], ident[:, :])
                    last.then_inc(sa["T"], 1)
                if q.live(-1):
                    pe.wait_ge(sa["msg"], q.at(-1, 1, 1))
                    j = q.slot(-1)
                    for t in range(T):
                        last = nc.tensor.matmul(bank[j][:, 0:HEADS * (HC + 1)], a_hot[:, j, t, :],
                                                a_msg[:, j, t, :], start=(t == 0), stop=(t == T - 1))
                    last.then_inc(sa["pv"], 1)
            run_steps(pe, GAT, 2, 3, body)

        @block.vector
        def _(dve):
            V = nc.vector
            chain = Chain(dve, s_chain)
            V.memset(src_i[:, :], PAD_NODE).then_inc(s_fill, 1)
            V.memset(dst_i[:, :], PAD_NODE).then_inc(s_fill, 1)
            V.memset(type_i[:, :], 0).then_inc(s_fill, 1)
            V.memset(w_f[:, :], 0.0).then_inc(s_fill, 1)
            V.memset(xs[:, FULL, :], 0.0).then_inc(s_fill, 1)
            V.memset(gcn_rec[:, :, :], 0.0).then_inc(s_fill, 1)
            V.memset(gat_rec[:, :, :], 0.0).then_inc(s_fill, 1)
            dve.wait_ge(s_fill, 7)
            V.memset(gcn_rec[:, :, 1:2], NO_NODE).then_inc(s_fill, 1)
            V.memset(gat_rec[:, :, 1:2], NO_NODE).then_inc(s_fill, 1)
            V.memset(zeros[:, :], 0.0).then_inc(s_fill, 1)

            def split(node_i, s, lo):
                chain(V.tensor_scalar(tmp_i[:, :], node_i[:, :], 7, None, ALU.logical_shift_right))
                chain(V.tensor_copy(block_of[s][:, :], tmp_i[:, :]))
                chain(V.tensor_scalar(tmp_i[:, :], node_i[:, :], P - 1, None, ALU.bitwise_and))
                chain(V.tensor_scalar(rank[:, :], block_of[s][:, :], float(NB), -4.0 * P,
                                      ALU.is_equal, ALU.mult))
                chain(V.tensor_tensor(lo, tmp_i[:, :], rank[:, :], ALU.add))

            def places(s, plan, block_row):
                key = block_of[s]
                for b in range(NBINS):
                    chain(V.tensor_scalar(mask[:, :], key[:, :], float(b), None, ALU.is_equal, ALU.add,
                                          accum_out=bins[:, 0, b:b + 1]))
                dve.sem_inc(s_pre, 1)
                dve.wait_ge(s_pfx, s + 1)
                per = plan.tiles * P
                chain(V.tensor_scalar(bins[:, 1, :], bank[1][:, 64:64 + NBINS], float(per - 1), None, ALU.add))
                chain(V.tensor_copy(bins_i[:, :], bins[:, 1, :]))
                chain(V.tensor_scalar(bins_i[:, :], bins_i[:, :], plan.shift, None, ALU.logical_shift_right))
                chain(V.tensor_copy(bins[:, 2, :], bins_i[:, :]))
                chain(V.tensor_tensor_scan(bins[:, 3, :], bins[:, 2, :], zeros[:, 0:NBINS], 0.0,
                                           ALU.add, ALU.add))
                chain(V.tensor_tensor(bins[:, 4, :], bins[:, 3, :], bins[:, 2, :], ALU.subtract))
                dve.sem_inc(s_scol, 1)
                chain(V.tensor_scalar(bins[:, 5, :], bins[:, 4, :], float(per), -1.0, ALU.mult, ALU.add))
                chain(V.tensor_tensor(bins[:, 6, :], bins[:, 5, :], bank[1][:, 0:NBINS], ALU.add))
                for b in range(NBINS):
                    chain(V.tensor_scalar(mask[:, :], key[:, :], float(b), None, ALU.is_equal))
                    chain(V.tensor_tensor_scan(rank[:, :], mask[:, :], zeros[:, :], bins[:, 6, b:b + 1],
                                               ALU.add, ALU.add))
                    chain(V.copy_predicated(place[:, :], mask[:, :], rank[:, :]))
                chain(V.tensor_copy(place_u[s][:, :], place[:, :]))
                chain(V.tensor_scalar(tmp_i[:, :], place_u[s][:, :].bitcast(I32), 7, None,
                                      ALU.logical_shift_right))
                chain(V.tensor_copy(rank[:, :], tmp_i[:, :]))
                chain(V.tensor_scalar(tmp_i[:, :], place_u[s][:, :].bitcast(I32), P - 1, None,
                                      ALU.bitwise_and))
                chain(V.tensor_copy(place[:, :], tmp_i[:, :]))
                chain(V.scalar_tensor_tensor(place_u[s][:, :], place[:, :], float(plan.slots), rank[:, :],
                                             ALU.mult, ALU.add))
                dve.sem_inc(s_place, 1)
                dve.wait_ge(s_scol2, s + 1)
                chain(V.tensor_copy(start_col[:, :], bank[0][0:NB, 500:501]))
                chain(V.tensor_scalar(passed[:, :], iota_n[0:NB, :], start_col[:, 0:1], None, ALU.is_ge))
                dve.sem_inc(s_pass, 1)
                dve.wait_ge(s_pass2, s + 1)
                half = GCN.groups // 2
                V.tensor_scalar(block_row[:, 0:half + 1], bank[0][0:1, 0:half + 1], -1.0, None, ALU.add)
                chain(V.tensor_scalar(block_row[:, half + 1:], bank[5][0:1, 0:GCN.groups - half - 1],
                                      -1.0, None, ALU.add))

            dve.wait_ge(s_in["src"], 32)
            split(src_i, 0, rec_src[0][:, :, 1])
            dve.wait_ge(s_in["dst"], 32)
            split(dst_i, 1, dst_lo[:, :])
            dve.wait_ge(s_in["type"], 32)
            dve.wait_ge(s_in["weight"], 32)
            chain(V.tensor_copy(rec_src[0][:, :, 2], w_f[:, :]))
            chain(V.scalar_tensor_tensor(rank[:, :], dst_i[:, :], float(N_TYPES), type_i[:, :],
                                         ALU.mult, ALU.add))
            chain(V.tensor_scalar(rec_src[0][:, :, 0], rank[:, :], float(NB * P * N_TYPES - 1), None, ALU.min))
            chain(V.tensor_scalar(rec_src[1][:, :, 0], src_i[:, :], float(NB * P - 1), None, ALU.min))
            chain(V.tensor_copy(rec_src[1][:, :, 1], dst_lo[:, :]))
            dve.wait_ge(s_const, 2)
            dve.wait_ge(s_fill, 10)
            places(0, GCN, gcn_block)

            def hots(i, h):
                col = i * (2 * HIST) + h * HIST
                lo = dst_lo[:, bass.ds(col, HIST)].unsqueeze(2)
                hi = block_of[1][:, bass.ds(col, HIST)].unsqueeze(2)
                V.tensor_tensor(lo_hot[:, h, :, :], spread(iota[:, :].unsqueeze(1), [P, HIST, P]),
                                spread(lo, [P, HIST, P]), ALU.is_equal)
                V.tensor_tensor(hi_hot[:, h, :, :], spread(iota[:, 0:NB].unsqueeze(1), [P, HIST, NB]),
                                spread(hi, [P, HIST, NB]), ALU.is_equal).then_inc(s_hot, 1)
            for h in range(2):
                hots(0, h)
            with dve.Fori(1, COLS // (2 * HIST)) as i:
                for h in range(2):
                    dve.wait_ge(s_cnt, i * 2 + h)
                    hots(i, h)
            dve.wait_ge(s_cnt, 2 * (COLS // (2 * HIST)) + 2)
            deg = bank[1][:, 256:256 + NB]
            chain(V.tensor_scalar(inv_deg[:, :], deg, 1.0, None, ALU.max))
            chain(V.tensor_scalar(deg_mask[:, :], deg, 0.0, None, ALU.is_gt))
            dve.sem_inc(s_sqrt, 1)
            dve.wait_ge(s_sqrt, 2)
            chain(V.reciprocal(inv_deg[:, :], inv_deg[:, :]))
            chain(V.tensor_tensor(inv_deg[:, :], inv_deg[:, :], deg_mask[:, :], ALU.mult))
            dve.sem_inc(s_z[0], 1)

            def row0(b):
                dve.wait_ge(s_tm[0], b + 1)
                if b >= 4:
                    dve.wait_ge(s_tw[b % 4], 16 * (b // 4))
                V.tensor_scalar(rows[:, b % 4, :], bank[2 + b % 2][:, :], inv_deg[:, b:b + 1], None,
                                ALU.mult).then_inc(s_tr[0], 1)
            for b in range(NB):
                dve.wait_ge(s_tT[0], b + 1)
                V.tensor_copy(nodeT[:, b % 2, :], bank[4 + b % 2][:, 0:P]
                              ).then_inc(s_tc[0], 1)
                if b >= 1:
                    row0(b - 1)
            row0(NB - 1)
            places(1, GAT, gat_block)

            for s in range(2):
                for h in range(2):
                    dve.wait_ge(s_sct[s][h], 16 * SCATTER * (COLS // (2 * SCATTER)))
            dve.wait_ge(s_recs_load, 32)
            dve.wait_ge(s_in["bias"], 64)
            dve.wait_ge(s_in["att"], 32)

            sums = acc[:, :, 0:D]

            def layer_gcn(layer):
                add = s_gadd[layer]
                V.memset(sums, 0.0).then_inc(add, 1)

                def body(q):
                    if q.live(1):
                        j = q.slot(1)
                        dve.wait_ge(s_stage[layer], q.at(1, 2, 2))
                        for t in range(GCN.step_tiles):
                            last = V.tensor_scalar(g_hot[:, j, t, :], iota[:, :], g_lw[:, j, t, 0:1],
                                                   g_lw[:, j, t, 1:2], ALU.is_equal, ALU.mult)
                        last.then_inc(s_ghot[layer], 1)
                    if q.live(2):
                        j = q.slot(2)
                        at = bass.ds(q.at(2, GCN.step_tiles), GCN.step_tiles)
                        V.tensor_copy(g_idx[:, j, :], gcn_rec[:, at, 0]).then_inc(s_stage[layer], 1)
                        V.tensor_copy(g_lw[:, j, :, :], gcn_rec[:, at, 1:3]).then_inc(s_stage[layer], 1)
                    if q.live(0):
                        wait_apart(dve, s_gpe[layer], q.at(0, GCN.part, GCN.part), s_apart[1])
                        for g in range(GCN.part):
                            b = dve.value_load(gcn_block[0:1, bass.ds(q.at(0, GCN.part, g), 1)],
                                               min_val=0, max_val=NB - 1)
                            dst_ap = acc[:, bass.ds(b, 1), 0:D]
                            dve.wait_ge(add, q.at(0, GCN.part, g + 1))
                            V.tensor_tensor(dst_ap, dst_ap, bank[g][:, 0:D].unsqueeze(1), ALU.add
                                            ).then_inc(add, 1)
                run_steps(dve, GCN, 0, 2, body)
                dve.wait_ge(add, GCN.groups + 1)
                if layer == 0:
                    chunks = 7
                C = 7
                for c in range(NB // C):
                    cs = slice(c * C, (c + 1) * C)
                    chain(V.tensor_tensor(z[:, cs, :], acc[:, cs, 0:D],
                                          spread(inv_deg[:, cs].unsqueeze(2), [P, C, D]), ALU.mult))
                    chain(V.tensor_tensor(z[:, cs, :], z[:, cs, :],
                                          spread(bias[:, layer, :].unsqueeze(1), [P, C, D]), ALU.add))
                    chain(V.scalar_tensor_tensor(z[:, cs, :], z[:, cs, :], 0.01, z[:, cs, :],
                                                 ALU.mult, ALU.max))
                    if layer < 2:
                        dve.sem_inc(s_z[layer + 1], C)
                chain(V.tensor_tensor(xs[:, :, :], xs[:, :, :], z[:, :, :], ALU.add))

            for layer in range(3):
                layer_gcn(layer)

            def layernorm(dst_t, n):
                for b in range(NB):
                    last = V.bn_stats(stats[:, b, :], xs[:, b, :])
                chain(last)
                for b in range(NB):
                    last = V.bn_aggr(mv[:, b, :], stats[:, b, :])
                chain(last)
                chain(V.tensor_scalar(mv[:, :, 1], mv[:, :, 1], 1e-5, None, ALU.add))
                dve.sem_inc(s_ln, 1)
                dve.wait_ge(s_ln2, n)
                chain(V.reciprocal(mv[:, :, 1], mv[:, :, 1]))
                for b in range(NB):
                    last = V.tensor_scalar(dst_t[:, b, :], xs[:, b, :], mv[:, b, 0:1], mv[:, b, 1:2],
                                           ALU.subtract, ALU.mult)
                chain(last)

            dve.sem_inc(s_xr, 1)
            dve.wait_ge(s_in["x"], 64)
            chain(V.scalar_tensor_tensor(xs[:, :, :], xs[:, :, :], 0.25, z[:, :, :], ALU.mult, ALU.add))
            layernorm(xs, 1)
            chain(V.scalar_tensor_tensor(z[:, :, :], xs[:, :, :], 0.0, xs[:, :, :], ALU.not_equal, ALU.mult))
            dve.sem_inc(s_z[3], NB)

            rows_v = rows[:, :, 0:HEADS * (HC + 1)].rearrange("p k (h c) -> p k h c", h=HEADS)
            acc_v = acc[:, :, :].rearrange("p b (h c) -> p b h c", h=HEADS)
            for k in range(4):
                dve.wait_ge(s_tw[k], 16 * tw_before(3, k))
            chain(V.memset(rows_v[:, :, :, HC:HC + 1], 1.0))
            for b in range(NB):
                k = b % 4
                dve.wait_ge(s_tm[3], b + 1)
                if b >= 4:
                    dve.wait_ge(s_tw[k], 16 * (tw_before(3, k) + b // 4))
                xp = bank[2 + b % 2][:, 0:D]
                V.tensor_copy(rows_v[:, k, :, 0:HC], xp.rearrange("p (h c) -> p h c", h=HEADS))
                chain(V.tensor_tensor(att_tmp[:, b % 2, :, :], spread(xp.unsqueeze(1), [P, 2, D]), att[:, :, :],
                                      ALU.mult))
                chain(V.tensor_reduce(state[:, b, 1:3, :],
                                      att_tmp[:, b % 2, :, :].rearrange("p s (h c) -> p s h c", h=HEADS),
                                      AX.X, ALU.add))
                V.tensor_copy(state[:, b, 0, :], state[:, b, 1, :])
                V.tensor_copy(acc[:, b, :], rows[:, k, 0:HEADS * (HC + 1)])
                V.tensor_copy(rows[:, k, ROW - HEADS:ROW], state[:, b, 1, :]).then_inc(s_tr[3], 1)
            dve.wait_ge(s_tr[3], NB)
            first = z[:, :, 0:HEADS]
            chain(V.tensor_tensor(first, state[:, :, 0, :], state[:, :, 2, :], ALU.add))
            chain(V.scalar_tensor_tensor(state[:, :, 1, :], first, 0.2, first, ALU.mult, ALU.max))
            dve.sem_inc(sa["add"], 1)

            def body(q):
                if q.live(3):
                    j = q.slot(3)
                    at = bass.ds(q.at(3, T), T)
                    V.tensor_copy(a_idx[:, j, :], gat_rec[:, at, 0])
                    V.tensor_copy(a_lo[:, j, :], gat_rec[:, at, 1]).then_inc(sa["stage"], 1)
                if q.live(2):
                    j = q.slot(2)
                    dve.wait_ge(sa["stage"], q.at(2, 1, 1))
                    for t in range(T):
                        last = V.tensor_scalar(a_hide[:, j, t, :], iota[:, :], a_lo[:, j, t:t + 1], -BIG,
                                               ALU.not_equal, ALU.mult)
                    last.then_inc(sa["hide"], 1)
                if q.live(1):
                    j = q.slot(1)
                    dve.wait_ge(sa["T"], q.at(1, 1, 1))
                    V.tensor_reduce(a_max[:, j, :], wide[:, :, :, :].rearrange("p h t e -> p h (t e)"),
                                    AX.X, ALU.max).then_inc(sa["m"], 1)
                    b = dve.value_load(gat_block[0:1, bass.ds(q.at(1), 1)], min_val=0, max_val=NB - 1)
                    st = [state[:, bass.ds(b, 1), k, :] for k in range(3)]
                    dve.wait_ge(sa["m"], q.at(1, 6, 1))
                    V.tensor_tensor(st[0], st[0], a_max[:, j, :].unsqueeze(1), ALU.max).then_inc(sa["m"], 1)
                    dve.wait_ge(sa["m"], q.at(1, 6, 2))
                    V.tensor_tensor(a_sum[:, j, :].unsqueeze(1), st[0], st[2], ALU.add).then_inc(sa["m"], 1)
                    dve.wait_ge(sa["m"], q.at(1, 6, 3))
                    V.scalar_tensor_tensor(a_node[:, j, HEADS:], a_sum[:, j, :], 0.2, a_sum[:, j, :],
                                           ALU.mult, ALU.max).then_inc(sa["m"], 1)
                    V.tensor_copy(a_node[:, j, 0:HEADS].unsqueeze(1), st[2])
                    dve.wait_ge(sa["m"], q.at(1, 6, 4))
                    V.tensor_tensor(a_drop[:, j, :].unsqueeze(1), st[1], a_node[:, j, HEADS:].unsqueeze(1),
                                    ALU.subtract).then_inc(sa["m"], 1)
                    dve.wait_ge(sa["m"], q.at(1, 6, 5))
                    V.tensor_scalar(st[1], a_node[:, j, HEADS:].unsqueeze(1), 1.0, None, ALU.mult
                                    ).then_inc(sa["m"], 1)
                if q.live(0):
                    j = q.slot(0)
                    dve.wait_ge(sa["node"], q.at(0, 1, 1))
                    n = bank[5][:, j * T * 4:(j + 1) * T * 4].rearrange("p (t k) -> p t k", k=4)
                    V.tensor_tensor(a_z[:, j, :, :], n[:, :, 0:HEADS], a_rows[:, j, :, ROW - HEADS:ROW],
                                    ALU.add).then_inc(sa["e"], 1)
                    dve.wait_ge(sa["e"], q.at(0, 3, 1))
                    V.scalar_tensor_tensor(a_l[:, j, :, :], a_z[:, j, :, :], 0.2, a_z[:, j, :, :],
                                           ALU.mult, ALU.max).then_inc(sa["e"], 1)
                    dve.wait_ge(sa["e"], q.at(0, 3, 2))
                    V.tensor_tensor(a_e[:, j, :, :], a_l[:, j, :, :], n[:, :, HEADS:], ALU.subtract
                                    ).then_inc(sa["e"], 1)
                if q.live(-1):
                    j = q.slot(-1)
                    dve.wait_ge(sa["p"], q.at(-1, 1, 1))
                    V.tensor_tensor(
                        a_msg[:, j, :, :].rearrange("p t (h c) -> p (t h) c", h=HEADS),
                        a_rows[:, j, :, 0:ROW - HEADS].rearrange("p t (h c) -> p t h c", h=HEADS),
                        spread(a_p[:, j, :, :].unsqueeze(3), [P, T, HEADS, HC + 1]), ALU.mult
                    ).then_inc(sa["msg"], 1)
                if q.live(-2):
                    j = q.slot(-2)
                    dve.wait_ge(sa["scale"], q.at(-2, 1, 1))
                    wait_apart(dve, sa["pv"], q.at(-2, 1, 1), s_apart[1])
                    b = dve.value_load(gat_block[0:1, bass.ds(q.at(-2), 1)], min_val=0, max_val=NB - 1)
                    dve.wait_ge(sa["add"], q.at(-2, 1, 1))
                    for h in range(HEADS):
                        hs = slice(h * (HC + 1), (h + 1) * (HC + 1))
                        part = acc[:, bass.ds(b, 1), hs]
                        last = V.scalar_tensor_tensor(part, part, a_scale[:, j, h:h + 1],
                                                      bank[j][:, hs].unsqueeze(1), ALU.mult, ALU.add)
                    last.then_inc(sa["add"], 1)
            run_steps(dve, GAT, 2, 3, body)
            dve.wait_ge(sa["add"], GAT.steps + 1)

            den = z[:, :, 0:HEADS]
            chain(V.tensor_scalar(den, acc_v[:, :, :, HC], 1e-16, None, ALU.add))
            chain(V.reciprocal(den, den))
            for h in range(HEADS):
                chain(V.tensor_tensor(acc_v[:, :, h, 0:HC], acc_v[:, :, h, 0:HC],
                                      spread(z[:, :, h:h + 1], [P, NB, HC]), ALU.mult))
            for h in range(HEADS):
                chain(V.tensor_tensor(acc_v[:, :, h, 0:HC], acc_v[:, :, h, 0:HC],
                                      spread(bias[:, 3, h * HC:(h + 1) * HC].unsqueeze(1), [P, NB, HC]),
                                      ALU.add))
            for h in range(HEADS):
                hs = slice(h * HC, (h + 1) * HC)
                chain(V.tensor_tensor(xs[:, :, hs], xs[:, :, hs], acc_v[:, :, h, 0:HC], ALU.add))
            layernorm(xs, 2)
            dve.sem_inc(s_fin, 1)


_INS = ["x", "src", "dst", "edge_type_4", "edge_weight", "L0_gnn_W1", "L0_gnn_b1", "L0_gnn_W2",
        "L0_gnn_b2", "L0_gnn_W3", "L0_gnn_b3", "L1_gnn_W", "L1_gnn_att_src", "L1_gnn_att_dst",
        "L1_gnn_bias"]


def kernel(**inputs):
    import numpy as _np
    import concourse.bacc as _bacc
    from concourse import mybir as _mybir
    from concourse.bass_utils import run_bass_kernel_spmd as _run

    nc = _bacc.Bacc("TRN2", target_bir_lowering=False, num_devices=1)
    arrays, args = {}, []
    for name in _INS:
        a = _np.ascontiguousarray(inputs[name])
        arrays[f"in_{name}"] = a
        args.append(nc.dram_tensor(f"in_{name}", a.shape, _mybir.dt.from_np(a.dtype),
                                   kind="ExternalInput").ap())
    out = nc.dram_tensor("out_x", (N_NODES, D), F32, kind="ExternalOutput").ap()
    gnn_kernel(nc, *args, out)
    r = _run(nc, [arrays], core_ids=[0])
    return r.results[0]["out_x"]
```

```python
from contextlib import ExitStack

import concourse.bass as bass
from concourse import mybir

F32, BF16 = mybir.dt.float32, mybir.dt.bfloat16
I32, U32, U8 = mybir.dt.int32, mybir.dt.uint32, mybir.dt.uint8
ALU = mybir.AluOpType
ACT = mybir.ActivationFunctionType
AX = mybir.AxisListType

P = 128
N_NODES, D, N_EDGES, N_TYPES, HEADS = 6250, 128, 206250, 4, 2
HC = D // HEADS
NB = -(-N_NODES // P)
FULL, REST = N_NODES // P, N_NODES % P
PAD_NODE = NB * P
NBINS = NB + 1
COLS = -(-N_EDGES // P)
LAST_COLS = N_EDGES - (P - 1) * COLS
SCATTER = 31
HIST = 13
EDGES_PAD = P * COLS
BIG = 2.0 ** 100
NO_NODE = -1.0


class Plan:

    def __init__(self, tiles, part, ring):
        self.tiles, self.part, self.ring = tiles, part, ring
        per = tiles * P
        most = (N_EDGES + NB * (per - 1)) // per
        self.steps = -(-most // part)
        self.groups = self.steps * part
        self.step_tiles = tiles * part
        self.slots = max(self.groups * tiles, (most + 1) * tiles)
        self.shift = per.bit_length() - 1


GCN = Plan(tiles=2, part=5, ring=3)
GAT = Plan(tiles=4, part=1, ring=6)
ROW = HEADS * (HC + 1) + HEADS
STATE = 3 * HEADS


class Step:

    def __init__(self, plan, base, i=None):
        self.plan, self.base, self.i = plan, base, i

    def live(self, lag):
        return self.i is not None or 0 <= self.base + lag < self.plan.steps

    def slot(self, lag):
        return (self.base + lag) % self.plan.ring

    def at(self, lag, times=1, plus=0):
        c = (self.base + lag) * times + plus
        return c if self.i is None else self.i * (self.plan.ring * times) + c

    def landed(self, lag, earlier=0, dmas=1):
        c = 16 * dmas * ((self.base + lag) // self.plan.ring + 1 + earlier)
        return c if self.i is None else self.i * (16 * dmas) + c


def run_steps(eng, plan, behind, ahead, body):
    whole = (plan.steps - ahead - behind) // plan.ring
    start, end = behind, behind + whole * plan.ring
    for q in range(-ahead, start):
        body(Step(plan, q))
    with eng.Fori(0, whole) as i:
        for j in range(plan.ring):
            body(Step(plan, start + j, i))
    for q in range(end, plan.steps + behind):
        body(Step(plan, q))


def wait_apart(eng, sem, value, count):
    eng.wait_ge(sem, value)
    eng.sem_inc(count, 1)


class Chain:

    def __init__(self, eng, sem):
        self.eng, self.sem, self.n = eng, sem, 0

    def __call__(self, ins):
        ins.then_inc(self.sem, 1)
        self.n += 1
        self.eng.wait_ge(self.sem, self.n)


def gnn_kernel(nc, x, src, dst, etype, weight, w1, b1, w2, b2, w3, b3, w_gat, att_src, att_dst,
               bias_gat, out):
    ctx = ExitStack()
    with ctx:
        def sb(name, shape, dt=F32, scope=ctx):
            return scope.enter_context(nc.sbuf_tensor(name, shape, dt))

        def sem(name):
            return ctx.enter_context(nc.semaphore(name))

        gcn_slots = nc.dram_tensor("gcn_slots", [P * GCN.slots, 3], F32).ap()
        by_dst = [nc.dram_tensor(f"by_dst_{n}", [EDGES_PAD + GAT.tiles * P, 1], I32).ap()
                  for n in ("src", "dst")]
        gcn_table = nc.dram_tensor("gcn_table", [NB * P * N_TYPES, D], F32).ap()
        gat_table = nc.dram_tensor("gat_table", [NB * P, ROW], F32).ap()

        iota = sb("iota", [P, P])
        iota_b = sb("iota_b", [P, P], BF16)
        iota_n = sb("iota_n", [P, GCN.groups])
        ident = sb("ident", [P, P])
        before = sb("before", [P, P])
        ones = sb("ones", [P, P])
        zeros = sb("zeros", [P, COLS], BF16)
        w_all = sb("w_all", [P, 3, N_TYPES * D])
        w_att = sb("w_att", [P, D])
        bias = sb("bias", [P, 4, D])
        att = sb("att", [P, 2, D])
        inv_deg = sb("inv_deg", [P, NB])
        deg_mask = sb("deg_mask", [P, NB])
        falls_i = sb("falls_i", [1, 1], I32)
        gcn_block = sb("gcn_block", [1, GCN.groups], I32)
        gat_block = sb("gat_block", [1, GAT.groups], I32)
        gat_edge = sb("gat_edge", [1, GAT.groups], I32)
        gat_base = sb("gat_base", [P, GAT.groups])
        gcn_rec = sb("gcn_rec", [P, GCN.slots, 3])
        xs = sb("xs", [P, NB, D])
        stats = sb("stats", [P, NB, 6])
        mv = sb("mv", [P, NB, 2])
        nodeT = sb("nodeT", [P, 2, P])
        rows = sb("rows", [P, 4, N_TYPES * D])

        sort = ExitStack()
        src_i = sb("src_i", [P, COLS], I32, sort)
        dst_i = sb("dst_i", [P, COLS], I32, sort)
        type_i = sb("type_i", [P, COLS], I32, sort)
        tmp_i = sb("tmp_i", [P, COLS], I32, sort)
        w_f = sb("w_f", [P, COLS], F32, sort)
        block_of = [sb(f"block_of{s}", [P, COLS], F32, sort) for s in range(2)]
        dst_lo = sb("dst_lo", [P, COLS], F32, sort)
        mask = sb("mask", [P, COLS], U8, sort)
        rank = sb("rank", [P, COLS], F32, sort)
        place = w_f
        place_u = [sb(f"place_u{s}", [P, COLS], U32, sort) for s in range(2)]
        gcn_src = sb("gcn_src", [P, COLS, 3], F32, sort)
        at_stage = [sb(f"at_stage{h}", [P, SCATTER], U32, sort) for h in range(2)]
        rec_stage = [sb(f"rec_stage{h}", [P, SCATTER * 3], F32, sort) for h in range(2)]
        pair_stage = [sb(f"pair_stage{n}", [P, SCATTER], I32, sort) for n in ("src", "dst")]
        dst_next = sb("dst_next", [P, 1], I32, sort)
        pads = sb("pads", [P, GAT.tiles], I32, sort)
        falls = sb("falls", [P, 4], F32, sort)
        lo_hot = sb("lo_hot", [P, 2, HIST, P], BF16, sort)
        hi_hot = sb("hi_hot", [P, 2, HIST, NB], BF16, sort)
        bins = sb("bins", [P, 8, NBINS], F32, sort)
        bins_i = sb("bins_i", [P, NBINS], I32, sort)
        start_col = sb("start_col", [NB, 2], F32, sort)
        passed = sb("passed", [NB, GCN.groups], F32, sort)
        sort.close()

        acc = sb("acc", [P, NB, HEADS * (HC + 1)])
        z = sb("z", [P, NB, D])
        gcn_scope = ExitStack()
        g_idx = sb("g_idx", [P, GCN.ring, GCN.step_tiles], U32, gcn_scope)
        g_lw = sb("g_lw", [P, GCN.ring, GCN.step_tiles, 2], F32, gcn_scope)
        g_rows = sb("g_rows", [P, GCN.ring, GCN.step_tiles, D], F32, gcn_scope)
        g_hot = sb("g_hot", [P, GCN.ring, GCN.step_tiles, P], F32, gcn_scope)
        gcn_scope.close()
        T, R = GAT.tiles, GAT.ring
        a_edge = sb("a_edge", [P, R, 2, T], I32)
        a_idx = sb("a_idx", [P, R, T], U32)
        a_lo = sb("a_lo", [P, R, T])
        a_rows = sb("a_rows", [P, R, T, ROW])
        a_hide = sb("a_hide", [P, R, T, P], BF16)
        a_hot = sb("a_hot", [P, R, T, P])
        a_cand = sb("a_cand", [P, 2, HEADS, T, P])
        a_hotT = sb("a_hotT", [P, R, T, P], BF16)
        a_msg = sb("a_msg", [P, R, T, HEADS * (HC + 1)])
        a_max = sb("a_max", [P, R, HEADS])
        a_sum = sb("a_sum", [P, R, HEADS])
        a_node = sb("a_node", [P, R, 2 * HEADS])
        a_part = sb("a_part", [P, R, 3, 2 * HEADS], BF16)
        a_left = sb("a_left", [P, R, 2 * HEADS])
        a_drop = sb("a_drop", [P, R, HEADS])
        a_scale = sb("a_scale", [P, R, HEADS])
        a_z = sb("a_z", [P, R, T, HEADS])
        a_l = sb("a_l", [P, R, T, HEADS])
        a_e = sb("a_e", [P, R, T, HEADS])
        a_p = sb("a_p", [P, R, T, HEADS])
        state = sb("state", [P, NB, 3, HEADS])
        att_tmp = sb("att_tmp", [P, 2, 2, D])

        bank = [ctx.enter_context(nc.psum_tensor(f"bank{k}", [P, 512], F32)) for k in range(4)]
        wide = ctx.enter_context(nc.psum_tensor("wide", [P, 2, HEADS, T, P], F32))
        bank += [wide[:, k // 2, k % 2, :, :].rearrange("p t e -> p (t e)") for k in range(4)]

        s_const, s_fill, s_chain = sem("s_const"), sem("s_fill"), sem("s_chain")
        s_in = {n: sem(f"s_in_{n}") for n in ("src", "dst", "type", "weight", "x", "w", "bias", "att", "next")}
        s_seed, s_recs, s_recs_load = sem("s_seed"), sem("s_recs"), sem("s_recs_load")
        s_pre = sem("s_pre")
        s_pfx = sem("s_pfx")
        s_scol, s_scol2 = sem("s_scol"), sem("s_scol2")
        s_pass, s_pass2 = sem("s_pass"), sem("s_pass2")
        s_place = sem("s_place")
        s_stg = [sem(f"s_stg{h}") for h in range(2)]
        s_sct = [sem(f"s_sct{h}") for h in range(2)]
        s_pair, s_pair_stage, s_paired = sem("s_pair"), sem("s_pair_stage"), sem("s_paired")
        s_falls, s_falls2, s_falls3 = sem("s_falls"), sem("s_falls2"), sem("s_falls3")
        s_hot, s_cnt = sem("s_hot"), sem("s_cnt")
        s_sqrt = sem("s_sqrt")
        s_sorted = sem("s_sorted")
        s_g = [sem(f"s_g{k}") for k in range(GCN.ring * GCN.step_tiles)]
        s_stage, s_ghot, s_gpe, s_gadd = ([sem(f"{n}{l}") for l in range(3)]
                                          for n in ("s_stage", "s_ghot", "s_gpe", "s_gadd"))
        s_z = [sem(f"s_z{l}") for l in range(4)]
        s_tT = [sem(f"s_tT{l}") for l in range(4)]
        s_tc = [sem(f"s_tc{l}") for l in range(4)]
        s_tm = [sem(f"s_tm{l}") for l in range(4)]
        s_tr = [sem(f"s_tr{l}") for l in range(4)]
        s_tw = [sem(f"s_tw{k}") for k in range(4)]
        s_ln, s_ln2 = sem("s_ln"), sem("s_ln2")
        s_xr = sem("s_xr")
        s_el = [sem(f"s_el{k}") for k in range(R)]
        sa = {n: sem(f"sa_{n}") for n in ("stage", "hide", "cand", "T", "hotT", "m", "scale", "node",
                                          "e", "p", "msg", "pv", "add", "max", "part")}
        s_ag = [sem(f"s_ag{k}") for k in range(R * T)]
        s_apart = [sem("s_apart_pool"), sem("s_apart_dve"), sem("s_apart_sp")]
        s_fin, s_out = sem("s_fin"), sem("s_out")

        def spread(ap, shape):
            return ap.to_broadcast(shape)

        block = ctx.enter_context(nc.Block())
        TABLE_TURNS = [NB] * 4

        def tw_before(layer, k):
            return layer * len(range(k, NB, 4))

        @block.sync
        def _(sp):
            def load_edges(name, dram, tile):
                flat = dram.rearrange("(o n) -> o n", o=1)
                body = flat[0:1, 0:(P - 1) * COLS].rearrange("o (p c) -> (o p) c", p=P - 1)
                sp.dma_start(tile[0:P - 1, :], body).then_inc(s_in[name], 16)
                sp.dma_start(tile[P - 1:P, 0:LAST_COLS], flat[0:1, (P - 1) * COLS:]).then_inc(s_in[name], 16)

            sp.wait_ge(s_fill, 4)
            load_edges("src", src, src_i)
            load_edges("dst", dst, dst_i)
            load_edges("type", etype, type_i)
            load_edges("weight", weight, w_f)
            sp.wait_ge(s_fill, 5)
            sp.dma_start(xs[:, 0:FULL, :],
                         x[0:FULL * P, :].rearrange("(b p) f -> p b f", p=P)).then_inc(s_in["x"], 16)
            sp.dma_start(xs[0:REST, FULL, :], x[FULL * P:, :]).then_inc(s_in["x"], 16)
            for l, w in enumerate((w1, w2, w3)):
                sp.dma_start(w_all[:, l, :].rearrange("i (t o) -> i t o", t=N_TYPES),
                             w.rearrange("t i o -> i t o")).then_inc(s_in["w"], 16)
            sp.dma_start(w_att[:, :], w_gat).then_inc(s_in["w"], 16)
            for l, b in enumerate((b1, b2, b3, bias_gat)):
                sp.dma_start(bias[:, l, :], b.partition_broadcast(P)).then_inc(s_in["bias"], 16)
            for l, a in enumerate((att_src, att_dst)):
                sp.dma_start(att[:, l, :], a.rearrange("h c -> (h c)").partition_broadcast(P)
                             ).then_inc(s_in["att"], 16)
            sp.wait_ge(s_fill, 9)
            sp.dma_start(dst_next[0:P - 1, :],
                         dst[COLS:].rearrange("(n o) -> n o", o=1)[0:(P - 2) * COLS + 1:COLS, :],
                         allow_slow_non_contiguous=True).then_inc(s_in["next"], 16)
            sp.dma_start(gcn_slots.rearrange("(p t) k -> p (t k)", p=P),
                         gcn_rec[:, :, :].rearrange("p t k -> p (t k)")).then_inc(s_seed, 16)
            for n in range(2):
                sp.dma_start(by_dst[n][EDGES_PAD:, 0].rearrange("(p t) -> p t", p=P), pads[:, :]
                             ).then_inc(s_seed, 16)

            def write_table(layer, table):
                for b in range(NB):
                    k = b % 4
                    sp.wait_ge(s_tr[layer], b + 1)
                    width = table.shape[1]
                    sp.dma_start(table[b * P:(b + 1) * P, :],
                                 rows[:, k, 0:width]).then_inc(s_tw[k], 16)

            gcn_wide = gcn_table.rearrange("(n t) f -> n (t f)", t=N_TYPES)
            write_table(0, gcn_wide)
            for h in range(2):
                sp.wait_ge(s_sct[h], 16 * SCATTER * (COLS // (2 * SCATTER)))
            sp.dma_start(gcn_rec[:, :, :].rearrange("p t k -> p (t k)"),
                         gcn_slots.rearrange("(p t) k -> p (t k)", p=P)).then_inc(s_recs_load, 16)
            write_table(1, gcn_wide)
            write_table(2, gcn_wide)
            sp.wait_ge(s_xr, 1)
            sp.dma_start(z[:, 0:FULL, :],
                         x[0:FULL * P, :].rearrange("(b p) f -> p b f", p=P)).then_inc(s_in["x"], 16)
            sp.dma_start(z[0:REST, FULL, :], x[FULL * P:, :]).then_inc(s_in["x"], 16)
            write_table(3, gat_table)
            sp.wait_ge(s_paired, 1)

            def body(q):
                if not q.live(0):
                    return
                e = sp.value_load(gat_edge[0:1, bass.ds(q.at(0), 1)], min_val=0, max_val=EDGES_PAD)
                if q.live(-R):
                    wait_apart(sp, sa["stage"], q.at(-R, 1, 1), s_apart[2])
                for n in range(2):
                    sp.dma_start(a_edge[:, q.slot(0), n, :],
                                 by_dst[n][bass.ds(e, T * P), 0].rearrange("(p t) -> p t", p=P)
                                 ).then_inc(s_el[q.slot(0)], 16)
            run_steps(sp, GAT, R, 0, body)
            sp.wait_ge(s_fin, 1)
            sp.dma_start(out[0:FULL * P, :].rearrange("(b p) f -> p b f", p=P),
                         xs[:, 0:FULL, :]).then_inc(s_out, 16)
            sp.dma_start(out[FULL * P:, :], xs[0:REST, FULL, :]).then_inc(s_out, 16)
            sp.wait_ge(s_out, 32)

        @block.gpsimd
        def _(pool):
            nc.gpsimd.iota(iota[:, :], [[1, P]], base=0, channel_multiplier=0,
                           allow_small_or_imprecise_dtypes=True)
            nc.gpsimd.iota(iota_b[:, :], [[1, P]], base=0, channel_multiplier=0,
                           allow_small_or_imprecise_dtypes=True)
            nc.gpsimd.iota(iota_n[:, :], [[1, GCN.groups]], base=0, channel_multiplier=0,
                           allow_small_or_imprecise_dtypes=True)
            nc.gpsimd.memset(ones[:, :], 1.0).then_inc(s_const, 1)
            pool.wait_ge(s_const, 1)
            nc.gpsimd.affine_select(out=ident[:, :], in_=ones[:, :], compare_op=ALU.is_equal, fill=0.0,
                                    base=0, pattern=[[1, P]], channel_multiplier=-1)
            nc.gpsimd.affine_select(out=before[:, :], in_=ones[:, :], compare_op=ALU.is_gt, fill=0.0,
                                    base=0, pattern=[[1, P]], channel_multiplier=-1).then_inc(s_const, 1)
            pool.wait_ge(s_seed, 48)
            with pool.Fori(0, COLS // (2 * SCATTER)) as i:
                for h in range(2):
                    wait_apart(pool, s_stg[h], i * 2 + 2, s_apart[0])
                    for c in range(SCATTER):
                        pool.indirect_dma_start(
                            out=gcn_slots, out_offset=bass.IndirectOffsetOnAxis(
                                ap=at_stage[h][:, c:c + 1], axis=0),
                            in_=rec_stage[h][:, c * 3:(c + 1) * 3], in_offset=None,
                        ).then_inc(s_sct[h], 16)

            pool.wait_ge(s_falls3, 1)
            pool.wait_ge(s_place, 2)
            for h in range(2):
                pool.wait_ge(s_sct[h], 16 * SCATTER * (COLS // (2 * SCATTER)))
            fell = pool.value_load(falls_i[0:1, 0:1], min_val=0, max_val=P)
            with pool.If(fell < 1):
                for n, tile in enumerate((src_i, dst_i)):
                    pool.dma_start(by_dst[n][0:EDGES_PAD, 0].rearrange("(p c) -> p c", p=P), tile[:, :]
                                   ).then_inc(s_pair, 16)
                pool.wait_ge(s_pair, 32)
            with pool.Else():
                with pool.Fori(0, COLS // SCATTER) as i:
                    at = bass.ds(i * SCATTER, SCATTER)
                    pool.tensor_copy(at_stage[0][:, :], place_u[1][:, at]).then_inc(s_pair_stage, 1)
                    for n, tile in enumerate((src_i, dst_i)):
                        pool.tensor_copy(pair_stage[n][:, :], tile[:, at]).then_inc(s_pair_stage, 1)
                    wait_apart(pool, s_pair_stage, i * 3 + 3, s_apart[0])
                    for n in range(2):
                        for c in range(SCATTER):
                            pool.indirect_dma_start(
                                out=by_dst[n], out_offset=bass.IndirectOffsetOnAxis(
                                    ap=at_stage[0][:, c:c + 1], axis=0),
                                in_=pair_stage[n][:, c:c + 1], in_offset=None,
                            ).then_inc(s_pair, 16)
                    wait_apart(pool, s_pair, i * (32 * SCATTER) + 32 * SCATTER, s_apart[0])
            pool.sem_inc(s_paired, 1)

            def gather_gcn(layer):
                for k in range(4):
                    pool.wait_ge(s_tw[k], 16 * tw_before(layer + 1, k))

                def body(q):
                    wait_apart(pool, s_stage[layer], q.at(0, 2, 2), s_apart[0])
                    for t in range(GCN.step_tiles):
                        pool.indirect_dma_start(
                            out=g_rows[:, q.slot(0), t, :], out_offset=None, in_=gcn_table,
                            in_offset=bass.IndirectOffsetOnAxis(
                                ap=g_idx[:, q.slot(0), t:t + 1], axis=0),
                        ).then_inc(s_g[q.slot(0) * GCN.step_tiles + t], 16)
                run_steps(pool, GCN, 0, 0, body)

            for layer in range(3):
                gather_gcn(layer)

            for k in range(4):
                pool.wait_ge(s_tw[k], 16 * tw_before(4, k))

            def body(q):
                wait_apart(pool, sa["stage"], q.at(0, 1, 1), s_apart[0])
                for t in range(T):
                    pool.indirect_dma_start(
                        out=a_rows[:, q.slot(0), t, :], out_offset=None, in_=gat_table,
                        in_offset=bass.IndirectOffsetOnAxis(ap=a_idx[:, q.slot(0), t:t + 1], axis=0),
                    ).then_inc(s_ag[q.slot(0) * T + t], 16)
            run_steps(pool, GAT, 0, 0, body)

        @block.scalar
        def _(act):
            act.wait_ge(s_place, 1)

            def stage(i, h):
                col = i * (2 * SCATTER) + h * SCATTER
                nc.scalar.copy(at_stage[h][:, :], place_u[0][:, bass.ds(col, SCATTER)]).then_inc(s_stg[h], 1)
                nc.scalar.copy(rec_stage[h][:, :].rearrange("p (c k) -> p c k", k=3),
                               gcn_src[:, bass.ds(col, SCATTER), :]).then_inc(s_stg[h], 1)
            for h in range(2):
                stage(0, h)
            turns = COLS // (2 * SCATTER)
            for first, end in ((1, turns // 2), (turns // 2, turns)):
                with act.Fori(first, end) as i:
                    for h in range(2):
                        act.wait_ge(s_sct[h], i * (16 * SCATTER))
                        stage(i, h)
                if first == 1:
                    act.wait_ge(s_sqrt, 1)
                    nc.scalar.sqrt(inv_deg[:, :], inv_deg[:, :]).then_inc(s_sqrt, 1)

            def table(layer):
                for b in range(NB):
                    act.wait_ge(s_tT[layer], b + 1)
                    nc.scalar.copy(nodeT[:, b % 2, :], bank[4 + b % 2][:, 0:P]
                                   ).then_inc(s_tc[layer], 1)
                    if b >= 1:
                        row(layer, b - 1)
                row(layer, NB - 1)

            def row(layer, b):
                act.wait_ge(s_tm[layer], b + 1)
                if b >= 4 or layer:
                    act.wait_ge(s_tw[b % 4], 16 * (tw_before(layer, b % 4) + b // 4))
                nc.scalar.activation(rows[:, b % 4, :], bank[2 + b % 2][:, :], ACT.Copy,
                                     scale=inv_deg[:, b:b + 1]).then_inc(s_tr[layer], 1)
            table(1)
            table(2)

            def ln_sqrt(n):
                act.wait_ge(s_ln, n)
                nc.scalar.sqrt(mv[:, :, 1], mv[:, :, 1]).then_inc(s_ln2, 1)

            ln_sqrt(1)
            for b in range(NB):
                act.wait_ge(s_tT[3], b + 1)
                nc.scalar.copy(nodeT[:, b % 2, :], bank[4 + b % 2][:, 0:P]
                               ).then_inc(s_tc[3], 1)

            def body(q):
                if q.live(1):
                    act.wait_ge(sa["max"], q.at(1, 1, 1))
                    nc.scalar.activation(a_hotT[:, q.slot(1), :, :], wide[:, q.slot(1) % 2, 0, :, :],
                                         ACT.Identity, bias=1.0, scale=1.0 / BIG).then_inc(sa["hotT"], 1)
                if q.live(3):
                    j, w = q.slot(3), q.slot(3) % 2
                    act.wait_ge(sa["hide"], q.at(3, 1, 1))
                    nc.scalar.activation(a_hot[:, j, :, :], a_hide[:, j, :, :], ACT.Identity,
                                         bias=1.0, scale=1.0 / BIG)
                    if q.live(1):
                        act.wait_ge(sa["T"], q.at(1, 1, 1))
                    for t in range(T):
                        act.wait_ge(s_ag[j * T + t], q.landed(3))
                        for h in range(HEADS):
                            last = nc.scalar.activation(
                                a_cand[:, w, h, t, :], a_hide[:, j, t, :], ACT.Identity,
                                bias=a_rows[:, j, t, ROW - HEADS + h:ROW - HEADS + h + 1])
                    last.then_inc(sa["cand"], 1)
                if q.live(1):
                    act.wait_ge(sa["m"], q.at(1, 5, 5))
                    nc.scalar.activation(a_scale[:, q.slot(1), :], a_drop[:, q.slot(1), :], ACT.Exp
                                         ).then_inc(sa["scale"], 1)
                if q.live(0):
                    act.wait_ge(sa["e"], q.at(0, 4, 4))
                    nc.scalar.activation(a_p[:, q.slot(0), :, :], a_e[:, q.slot(0), :, :], ACT.Exp
                                         ).then_inc(sa["p"], 1)

            run_steps(act, GAT, 2, 4, body)
            ln_sqrt(2)

        @block.tensor
        def _(pe):
            pe.wait_ge(s_const, 2)

            def ranks(s):
                pe.wait_ge(s_pre, s + 1)
                nc.tensor.matmul(bank[1][:, 0:NBINS], before[:, :], bins[:, 0, :], start=True, stop=True)
                nc.tensor.matmul(bank[1][:, 64:64 + NBINS], ones[:, :], bins[:, 0, :],
                                 start=True, stop=True).then_inc(s_pfx, 1)
                pe.wait_ge(s_scol, s + 1)
                for n, row in enumerate((4, 7)[:s + 1]):
                    last = nc.tensor.matmul(bank[0][0:NB, 500 + n:501 + n], bins[0:1, row, 0:NB],
                                            ones[0:1, 0:1], start=True, stop=True)
                last.then_inc(s_scol2, 1)
                pe.wait_ge(s_pass, s + 1)
                if s == 0:
                    half = GCN.groups // 2
                    nc.tensor.matmul(bank[0][0:1, 0:half + 1], ones[0:NB, 0:1], passed[:, 0:half + 1],
                                     start=True, stop=True)
                    nc.tensor.matmul(bank[5][0:1, 0:GCN.groups - half - 1], ones[0:NB, 0:1],
                                     passed[:, half + 1:], start=True, stop=True).then_inc(s_pass2, 1)
                else:
                    nc.tensor.matmul(bank[0][:, 0:GAT.groups], ones[0:NB, :], passed[:, 0:GAT.groups],
                                     start=True, stop=True)
                    nc.tensor.matmul(bank[5][0:1, 0:GAT.groups], start_col[:, 1:2], passed[:, 0:GAT.groups],
                                     start=True, stop=True).then_inc(s_pass2, 1)

            ranks(0)
            pe.wait_ge(s_hot, 1)
            nc.tensor.matmul(bank[1][:, 256:256 + NB], lo_hot[:, 0, 0, :], zeros[:, 0:NB],
                             start=True, stop=False).then_inc(s_cnt, 1)
            with pe.Fori(0, COLS // (2 * HIST)) as i:
                for h in range(2):
                    pe.wait_ge(s_hot, i * 2 + h + 1)
                    for c in range(HIST):
                        last = nc.tensor.matmul(bank[1][:, 256:256 + NB], lo_hot[:, h, c, :],
                                                hi_hot[:, h, c, :], start=False, stop=False,
)
                    last.then_inc(s_cnt, 1)
            nc.tensor.matmul(bank[1][:, 256:256 + NB], lo_hot[:, 0, 0, :], zeros[:, 0:NB],
                             start=False, stop=True).then_inc(s_cnt, 1)

            def table(layer, node, w, evicted):
                def product(b):
                    pe.wait_ge(s_tc[layer], b + 1)
                    if b >= 2:
                        pe.wait_ge(s_tr[layer], b - 1)
                    nc.tensor.matmul(bank[2 + b % 2][:, 0:w.shape[1]], nodeT[:, b % 2, :], w,
                                     start=True, stop=True).then_inc(s_tm[layer], 1)
                for b in range(NB):
                    pe.wait_ge(s_z[layer], b + 1 if layer else 1)
                    if b >= 2:
                        pe.wait_ge(s_tc[layer], b - 1)
                    nc.tensor.transpose(bank[4 + b % 2][:, 0:P], node[:, b, :], ident[:, :]
                                        ).then_inc(s_tT[layer], 1)
                    if b >= 1:
                        product(b - 1)
                product(NB - 1)

            pe.wait_ge(s_in["x"], 32)
            pe.wait_ge(s_in["w"], 64)
            table(0, xs, w_all[:, 0, :], None)
            ranks(1)
            pe.wait_ge(s_falls, 1)
            nc.tensor.matmul(bank[3][0:1, 0:1], falls[:, 3:4], ones[:, 0:1], start=True, stop=True
                             ).then_inc(s_falls2, 1)

            def sum_gcn(layer):
                def body(q):
                    j = q.slot(0)
                    pe.wait_ge(s_ghot[layer], q.at(0, 1, 1))
                    pe.wait_ge(s_gadd[layer], q.at(0, GCN.part, 1))
                    for g in range(GCN.part):
                        for t in range(GCN.tiles):
                            k = g * GCN.tiles + t
                            pe.wait_ge(s_g[j * GCN.step_tiles + k],
                                       q.landed(0, layer * len(range(j, GCN.steps, GCN.ring))))
                            last = nc.tensor.matmul(bank[g][:, 0:D], g_hot[:, j, k, :], g_rows[:, j, k, :],
                                                    start=(t == 0), stop=(t == GCN.tiles - 1))
                        last.then_inc(s_gpe[layer], 1)
                run_steps(pe, GCN, 0, 0, body)

            sum_gcn(0)
            table(1, z, w_all[:, 1, :], None)
            sum_gcn(1)
            table(2, z, w_all[:, 2, :], None)
            sum_gcn(2)
            table(3, z, w_att[:, :], None)

            def body(q):
                if q.live(2):
                    j, w = q.slot(2), q.slot(2) % 2
                    pe.wait_ge(sa["cand"], q.at(2, 1, 1))
                    if q.live(0):
                        pe.wait_ge(sa["hotT"], q.at(0, 1, 1))
                    for h in range(HEADS):
                        for t in range(T):
                            last = nc.tensor.transpose(wide[:, w, h, t, :], a_cand[:, w, h, t, :],
                                                       ident[:, :])
                    last.then_inc(sa["T"], 1)
                if q.live(-1):
                    pe.wait_ge(sa["msg"], q.at(-1, 1, 1))
                    if q.live(-4):
                        pe.wait_ge(sa["add"], q.at(-4, 1, 2))
                    j = q.slot(-1)
                    for t in range(T):
                        last = nc.tensor.matmul(bank[j % 3][:, 0:HEADS * (HC + 1)], a_hot[:, j, t, :],
                                                a_msg[:, j, t, :], start=(t == 0), stop=(t == T - 1))
                    last.then_inc(sa["pv"], 1)
                if q.live(1):
                    j = q.slot(1)
                    pe.wait_ge(sa["part"], q.at(1, 4, 4))
                    pe.wait_ge(sa["hotT"], q.at(1, 1, 1))
                    if q.live(0):
                        pe.wait_ge(sa["e"], q.at(0, 4, 3))
                    for t in range(T):
                        for k in range(3):
                            last = nc.tensor.matmul(bank[3][:, t * 4:(t + 1) * 4], a_hotT[:, j, t, :],
                                                    a_part[:, j, k, :], start=(k == 0), stop=(k == 2))
                    last.then_inc(sa["node"], 1)
            run_steps(pe, GAT, 2, 4, body)

        @block.vector
        def _(dve):
            V = nc.vector
            chain = Chain(dve, s_chain)
            V.memset(src_i[:, :], PAD_NODE).then_inc(s_fill, 1)
            V.memset(dst_i[:, :], PAD_NODE).then_inc(s_fill, 1)
            V.memset(type_i[:, :], 0).then_inc(s_fill, 1)
            V.memset(w_f[:, :], 0.0).then_inc(s_fill, 1)
            V.memset(xs[:, FULL, :], 0.0).then_inc(s_fill, 1)
            V.memset(gcn_rec[:, :, :], 0.0).then_inc(s_fill, 1)
            V.memset(pads[:, :], PAD_NODE).then_inc(s_fill, 1)
            dve.wait_ge(s_fill, 7)
            V.memset(gcn_rec[:, :, 1:2], NO_NODE).then_inc(s_fill, 1)
            V.memset(dst_next[:, :], PAD_NODE).then_inc(s_fill, 1)
            V.memset(zeros[:, :], 0.0).then_inc(s_fill, 1)

            def split(node_i, s, lo):
                chain(V.tensor_scalar(tmp_i[:, :], node_i[:, :], 7, None, ALU.logical_shift_right))
                chain(V.tensor_copy(block_of[s][:, :], tmp_i[:, :]))
                chain(V.tensor_scalar(tmp_i[:, :], node_i[:, :], P - 1, None, ALU.bitwise_and))
                chain(V.tensor_scalar(rank[:, :], block_of[s][:, :], float(NB), -4.0 * P,
                                      ALU.is_equal, ALU.mult))
                chain(V.tensor_tensor(lo, tmp_i[:, :], rank[:, :], ALU.add))

            def places(s, plan):
                key = block_of[s]
                for b in range(NBINS):
                    chain(V.tensor_scalar(mask[:, :], key[:, :], float(b), None, ALU.is_equal, ALU.add,
                                          accum_out=bins[:, 0, b:b + 1]))
                dve.sem_inc(s_pre, 1)
                dve.wait_ge(s_pfx, s + 1)
                per = plan.tiles * P
                lower, total = bank[1][:, 0:NBINS], bank[1][:, 64:64 + NBINS]
                chain(V.tensor_scalar(bins[:, 1, :], total, float(per - 1), None, ALU.add))
                chain(V.tensor_copy(bins_i[:, :], bins[:, 1, :]))
                chain(V.tensor_scalar(bins_i[:, :], bins_i[:, :], plan.shift, None, ALU.logical_shift_right))
                chain(V.tensor_copy(bins[:, 2, :], bins_i[:, :]))
                chain(V.tensor_tensor_scan(bins[:, 3, :], bins[:, 2, :], zeros[:, 0:NBINS], 0.0,
                                           ALU.add, ALU.add))
                chain(V.tensor_tensor(bins[:, 4, :], bins[:, 3, :], bins[:, 2, :], ALU.subtract))
                if s == 0:
                    chain(V.tensor_scalar(bins[:, 5, :], bins[:, 4, :], float(per), -1.0,
                                          ALU.mult, ALU.add))
                else:
                    chain(V.tensor_tensor_scan(bins[:, 3, :], total, zeros[:, 0:NBINS], -1.0,
                                               ALU.add, ALU.add))
                    chain(V.tensor_tensor(bins[:, 5, :], bins[:, 3, :], total, ALU.subtract))
                    chain(V.scalar_tensor_tensor(bins[:, 1, :], bins[:, 4, :], -float(per), bins[:, 5, :],
                                                 ALU.mult, ALU.add))
                    chain(V.tensor_scalar(bins[:, 1, :], bins[:, 1, :], 1.0, None, ALU.add))
                    chain(V.tensor_copy(bins[:, 7, 0:1], bins[:, 1, 0:1]))
                    chain(V.tensor_tensor(bins[:, 7, 1:], bins[:, 1, 1:], bins[:, 1, 0:NBINS - 1],
                                          ALU.subtract))
                dve.sem_inc(s_scol, 1)
                chain(V.tensor_tensor(bins[:, 6, :], bins[:, 5, :], lower, ALU.add))
                for b in range(NBINS):
                    chain(V.tensor_scalar(mask[:, :], key[:, :], float(b), None, ALU.is_equal))
                    chain(V.tensor_tensor_scan(rank[:, :], mask[:, :], zeros[:, :], bins[:, 6, b:b + 1],
                                               ALU.add, ALU.add))
                    chain(V.copy_predicated(place[:, :], mask[:, :], rank[:, :]))
                chain(V.tensor_copy(place_u[s][:, :], place[:, :]))
                if s == 0:
                    chain(V.tensor_scalar(tmp_i[:, :], place_u[s][:, :].bitcast(I32), 7, None,
                                          ALU.logical_shift_right))
                    chain(V.tensor_copy(rank[:, :], tmp_i[:, :]))
                    chain(V.tensor_scalar(tmp_i[:, :], place_u[s][:, :].bitcast(I32), P - 1, None,
                                          ALU.bitwise_and))
                    chain(V.tensor_copy(place[:, :], tmp_i[:, :]))
                    chain(V.scalar_tensor_tensor(place_u[s][:, :], place[:, :], float(plan.slots),
                                                 rank[:, :], ALU.mult, ALU.add))
                dve.sem_inc(s_place, 1)
                dve.wait_ge(s_scol2, s + 1)
                chain(V.tensor_copy(start_col[:, 0:s + 1], bank[0][0:NB, 500:501 + s]))
                chain(V.tensor_scalar(passed[:, :], iota_n[0:NB, :], start_col[:, 0:1], None, ALU.is_ge))
                dve.sem_inc(s_pass, 1)
                dve.wait_ge(s_pass2, s + 1)
                if s == 0:
                    half = GCN.groups // 2
                    chain(V.tensor_scalar(gcn_block[:, 0:half + 1], bank[0][0:1, 0:half + 1],
                                          -1.0, None, ALU.add))
                    chain(V.tensor_scalar(gcn_block[:, half + 1:], bank[5][0:1, 0:GCN.groups - half - 1],
                                          -1.0, None, ALU.add))
                else:
                    begun = bank[0][:, 0:GAT.groups]
                    chain(V.tensor_scalar(gat_block[:, :], begun[0:1, :], -1.0, None, ALU.add))
                    chain(V.tensor_scalar(gat_base[:, :], begun, float(P), -float(P), ALU.mult, ALU.add))
                    chain(V.scalar_tensor_tensor(passed[0:1, 0:GAT.groups], iota_n[0:1, 0:GAT.groups],
                                                 float(per), bank[5][0:1, 0:GAT.groups],
                                                 ALU.mult, ALU.add))
                    chain(V.tensor_scalar(gat_edge[:, :], passed[0:1, 0:GAT.groups], float(EDGES_PAD),
                                          None, ALU.min))

            dve.wait_ge(s_in["src"], 32)
            split(src_i, 0, gcn_src[:, :, 1])
            dve.wait_ge(s_in["dst"], 32)
            split(dst_i, 1, dst_lo[:, :])
            dve.wait_ge(s_in["type"], 32)
            dve.wait_ge(s_in["weight"], 32)
            chain(V.tensor_copy(gcn_src[:, :, 2], w_f[:, :]))
            chain(V.scalar_tensor_tensor(rank[:, :], dst_i[:, :], float(N_TYPES), type_i[:, :],
                                         ALU.mult, ALU.add))
            chain(V.tensor_scalar(gcn_src[:, :, 0], rank[:, :], float(NB * P * N_TYPES - 1), None, ALU.min))
            dve.wait_ge(s_const, 2)
            dve.wait_ge(s_fill, 10)
            places(0, GCN)

            def hots(i, h):
                col = i * (2 * HIST) + h * HIST
                lo = dst_lo[:, bass.ds(col, HIST)].unsqueeze(2)
                hi = block_of[1][:, bass.ds(col, HIST)].unsqueeze(2)
                V.tensor_tensor(lo_hot[:, h, :, :], spread(iota[:, :].unsqueeze(1), [P, HIST, P]),
                                spread(lo, [P, HIST, P]), ALU.is_equal)
                V.tensor_tensor(hi_hot[:, h, :, :], spread(iota[:, 0:NB].unsqueeze(1), [P, HIST, NB]),
                                spread(hi, [P, HIST, NB]), ALU.is_equal).then_inc(s_hot, 1)
            for h in range(2):
                hots(0, h)
            with dve.Fori(1, COLS // (2 * HIST)) as i:
                for h in range(2):
                    dve.wait_ge(s_cnt, i * 2 + h)
                    hots(i, h)
            dve.wait_ge(s_cnt, 2 * (COLS // (2 * HIST)) + 2)
            deg = bank[1][:, 256:256 + NB]
            chain(V.tensor_scalar(inv_deg[:, :], deg, 1.0, None, ALU.max))
            chain(V.tensor_scalar(deg_mask[:, :], deg, 0.0, None, ALU.is_gt))
            dve.sem_inc(s_sqrt, 1)
            dve.wait_ge(s_sqrt, 2)
            chain(V.reciprocal(inv_deg[:, :], inv_deg[:, :]))
            chain(V.tensor_tensor(inv_deg[:, :], inv_deg[:, :], deg_mask[:, :], ALU.mult))
            dve.sem_inc(s_z[0], 1)

            def row0(b):
                dve.wait_ge(s_tm[0], b + 1)
                if b >= 4:
                    dve.wait_ge(s_tw[b % 4], 16 * (b // 4))
                V.tensor_scalar(rows[:, b % 4, :], bank[2 + b % 2][:, :], inv_deg[:, b:b + 1], None,
                                ALU.mult).then_inc(s_tr[0], 1)
            for b in range(NB):
                dve.wait_ge(s_tT[0], b + 1)
                V.tensor_copy(nodeT[:, b % 2, :], bank[4 + b % 2][:, 0:P]
                              ).then_inc(s_tc[0], 1)
                if b >= 1:
                    row0(b - 1)
            row0(NB - 1)
            places(1, GAT)
            dve.wait_ge(s_in["next"], 16)
            chain(V.tensor_copy(rank[:, :], dst_i[:, :]))
            chain(V.tensor_tensor(place[:, 0:COLS - 1], rank[:, 0:COLS - 1], rank[:, 1:], ALU.is_gt))
            chain(V.tensor_reduce(falls[:, 0:1], place[:, 0:COLS - 1], AX.X, ALU.max))
            chain(V.tensor_copy(falls[:, 1:2], dst_next[:, :]))
            chain(V.tensor_tensor(falls[:, 2:3], rank[:, COLS - 1:], falls[:, 1:2], ALU.is_gt))
            chain(V.tensor_tensor(falls[:, 3:4], falls[:, 0:1], falls[:, 2:3], ALU.max))
            dve.sem_inc(s_falls, 1)
            dve.wait_ge(s_falls2, 1)
            chain(V.tensor_copy(falls_i[:, :], bank[3][0:1, 0:1]))
            dve.sem_inc(s_falls3, 1)

            dve.wait_ge(s_paired, 1)
            for h in range(2):
                dve.wait_ge(s_sct[h], 16 * SCATTER * (COLS // (2 * SCATTER)))
            dve.wait_ge(s_recs_load, 16)
            dve.wait_ge(s_in["bias"], 64)
            dve.wait_ge(s_in["att"], 32)

            sums = acc[:, :, 0:D]

            def layer_gcn(layer):
                add = s_gadd[layer]
                V.memset(sums, 0.0).then_inc(add, 1)

                def body(q):
                    if q.live(1):
                        j = q.slot(1)
                        dve.wait_ge(s_stage[layer], q.at(1, 2, 2))
                        for t in range(GCN.step_tiles):
                            last = V.tensor_scalar(g_hot[:, j, t, :], iota[:, :], g_lw[:, j, t, 0:1],
                                                   g_lw[:, j, t, 1:2], ALU.is_equal, ALU.mult)
                        last.then_inc(s_ghot[layer], 1)
                    if q.live(2):
                        j = q.slot(2)
                        at = bass.ds(q.at(2, GCN.step_tiles), GCN.step_tiles)
                        V.tensor_copy(g_idx[:, j, :], gcn_rec[:, at, 0]).then_inc(s_stage[layer], 1)
                        V.tensor_copy(g_lw[:, j, :, :], gcn_rec[:, at, 1:3]).then_inc(s_stage[layer], 1)
                    if q.live(0):
                        wait_apart(dve, s_gpe[layer], q.at(0, GCN.part, GCN.part), s_apart[1])
                        for g in range(GCN.part):
                            b = dve.value_load(gcn_block[0:1, bass.ds(q.at(0, GCN.part, g), 1)],
                                               min_val=0, max_val=NB - 1)
                            dst_ap = acc[:, bass.ds(b, 1), 0:D]
                            dve.wait_ge(add, q.at(0, GCN.part, g + 1))
                            V.tensor_tensor(dst_ap, dst_ap, bank[g][:, 0:D].unsqueeze(1), ALU.add
                                            ).then_inc(add, 1)
                run_steps(dve, GCN, 0, 2, body)
                dve.wait_ge(add, GCN.groups + 1)
                if layer == 0:
                    chunks = 7
                C = 7
                for c in range(NB // C):
                    cs = slice(c * C, (c + 1) * C)
                    chain(V.tensor_tensor(z[:, cs, :], acc[:, cs, 0:D],
                                          spread(inv_deg[:, cs].unsqueeze(2), [P, C, D]), ALU.mult))
                    chain(V.tensor_tensor(z[:, cs, :], z[:, cs, :],
                                          spread(bias[:, layer, :].unsqueeze(1), [P, C, D]), ALU.add))
                    chain(V.scalar_tensor_tensor(z[:, cs, :], z[:, cs, :], 0.01, z[:, cs, :],
                                                 ALU.mult, ALU.max))
                    if layer < 2:
                        dve.sem_inc(s_z[layer + 1], C)
                chain(V.tensor_tensor(xs[:, :, :], xs[:, :, :], z[:, :, :], ALU.add))

            for layer in range(3):
                layer_gcn(layer)

            def layernorm(dst_t, n):
                for b in range(NB):
                    last = V.bn_stats(stats[:, b, :], xs[:, b, :])
                chain(last)
                for b in range(NB):
                    last = V.bn_aggr(mv[:, b, :], stats[:, b, :])
                chain(last)
                chain(V.tensor_scalar(mv[:, :, 1], mv[:, :, 1], 1e-5, None, ALU.add))
                dve.sem_inc(s_ln, 1)
                dve.wait_ge(s_ln2, n)
                chain(V.reciprocal(mv[:, :, 1], mv[:, :, 1]))
                for b in range(NB):
                    last = V.tensor_scalar(dst_t[:, b, :], xs[:, b, :], mv[:, b, 0:1], mv[:, b, 1:2],
                                           ALU.subtract, ALU.mult)
                chain(last)

            dve.sem_inc(s_xr, 1)
            dve.wait_ge(s_in["x"], 64)
            chain(V.scalar_tensor_tensor(xs[:, :, :], xs[:, :, :], 0.25, z[:, :, :], ALU.mult, ALU.add))
            layernorm(xs, 1)
            chain(V.scalar_tensor_tensor(z[:, :, :], xs[:, :, :], 0.0, xs[:, :, :], ALU.not_equal, ALU.mult))
            dve.sem_inc(s_z[3], NB)

            rows_v = rows[:, :, 0:HEADS * (HC + 1)].rearrange("p k (h c) -> p k h c", h=HEADS)
            acc_v = acc[:, :, :].rearrange("p b (h c) -> p b h c", h=HEADS)
            for k in range(4):
                dve.wait_ge(s_tw[k], 16 * tw_before(3, k))
            chain(V.memset(rows_v[:, :, :, HC:HC + 1], 1.0))
            for b in range(NB):
                k = b % 4
                dve.wait_ge(s_tm[3], b + 1)
                if b >= 4:
                    dve.wait_ge(s_tw[k], 16 * (tw_before(3, k) + b // 4))
                xp = bank[2 + b % 2][:, 0:D]
                V.tensor_copy(rows_v[:, k, :, 0:HC], xp.rearrange("p (h c) -> p h c", h=HEADS))
                chain(V.tensor_tensor(att_tmp[:, b % 2, :, :], spread(xp.unsqueeze(1), [P, 2, D]), att[:, :, :],
                                      ALU.mult))
                chain(V.tensor_reduce(state[:, b, 1:3, :],
                                      att_tmp[:, b % 2, :, :].rearrange("p s (h c) -> p s h c", h=HEADS),
                                      AX.X, ALU.add))
                V.tensor_copy(state[:, b, 0, :], state[:, b, 1, :])
                V.tensor_copy(acc[:, b, :], rows[:, k, 0:HEADS * (HC + 1)])
                V.tensor_copy(rows[:, k, ROW - HEADS:ROW], state[:, b, 1, :]).then_inc(s_tr[3], 1)
            dve.wait_ge(s_tr[3], NB)
            first = z[:, :, 0:HEADS]
            chain(V.tensor_tensor(first, state[:, :, 0, :], state[:, :, 2, :], ALU.add))
            chain(V.scalar_tensor_tensor(state[:, :, 1, :], first, 0.2, first, ALU.mult, ALU.max))
            dve.sem_inc(sa["add"], 1)

            def body(q):
                if q.live(1):
                    m = q.slot(1)
                    b = dve.value_load(gat_block[0:1, bass.ds(q.at(1), 1)], min_val=0, max_val=NB - 1)
                    st = [state[:, bass.ds(b, 1), k, :] for k in range(3)]
                    dve.wait_ge(sa["T"], q.at(1, 1, 1))
                    V.tensor_reduce(a_max[:, m, :], wide[:, m % 2, :, :, :].rearrange("p h t e -> p h (t e)"),
                                    AX.X, ALU.max).then_inc(sa["max"], 1)
                if q.live(4):
                    j = q.slot(4)
                    dve.wait_ge(s_el[j], q.landed(4, 0, 2))
                    V.tensor_scalar(a_idx[:, j, :], a_edge[:, j, 0, :], float(NB * P - 1), None, ALU.min)
                    V.tensor_scalar(a_lo[:, j, :], a_edge[:, j, 1, :], gat_base[:, bass.ds(q.at(4), 1)],
                                    None, ALU.subtract).then_inc(sa["stage"], 1)
                if q.live(1):
                    dve.wait_ge(sa["max"], q.at(1, 1, 1))
                    V.tensor_tensor(st[0], st[0], a_max[:, m, :].unsqueeze(1), ALU.max).then_inc(sa["m"], 1)
                if q.live(0):
                    e = q.slot(0)
                    dve.wait_ge(sa["node"], q.at(0, 1, 1))
                    n = bank[3][:, 0:T * 4].rearrange("p (t k) -> p t k", k=4)
                    V.tensor_tensor(a_z[:, e, :, :], n[:, :, 0:HEADS], a_rows[:, e, :, ROW - HEADS:ROW],
                                    ALU.add).then_inc(sa["e"], 1)
                if q.live(3):
                    h = q.slot(3)
                    dve.wait_ge(sa["stage"], q.at(3, 1, 1))

                    def hide(t):
                        return V.tensor_scalar(a_hide[:, h, t, :], iota_b[:, :], a_lo[:, h, t:t + 1], -BIG,
                                               ALU.not_equal, ALU.mult)
                    hide(0)
                if q.live(1):
                    dve.wait_ge(sa["m"], q.at(1, 5, 1))
                    V.tensor_tensor(a_sum[:, m, :].unsqueeze(1), st[0], st[2], ALU.add).then_inc(sa["m"], 1)
                if q.live(0):
                    dve.wait_ge(sa["e"], q.at(0, 4, 1))
                    V.scalar_tensor_tensor(a_l[:, e, :, :], a_z[:, e, :, :], 0.2, a_z[:, e, :, :],
                                           ALU.mult, ALU.max).then_inc(sa["e"], 1)
                if q.live(3):
                    hide(1)
                if q.live(1):
                    dve.wait_ge(sa["m"], q.at(1, 5, 2))
                    V.tensor_scalar(a_node[:, m, 0:HEADS].unsqueeze(1), st[2], 1.0, None, ALU.mult)
                    V.scalar_tensor_tensor(a_node[:, m, HEADS:], a_sum[:, m, :], 0.2, a_sum[:, m, :],
                                           ALU.mult, ALU.max).then_inc(sa["m"], 1)
                    dve.wait_ge(sa["m"], q.at(1, 5, 3))
                    V.tensor_copy(a_part[:, m, 0, :], a_node[:, m, :]).then_inc(sa["part"], 1)
                if q.live(0):
                    dve.wait_ge(sa["e"], q.at(0, 4, 2))
                    V.tensor_tensor(a_l[:, e, :, :], a_l[:, e, :, :], n[:, :, HEADS:], ALU.subtract
                                    ).then_inc(sa["e"], 1)
                if q.live(3):
                    hide(2)
                if q.live(1):
                    dve.wait_ge(sa["part"], q.at(1, 4, 1))
                    V.tensor_tensor(a_left[:, m, :], a_node[:, m, :], a_part[:, m, 0, :], ALU.subtract
                                    ).then_inc(sa["part"], 1)
                    V.tensor_tensor(a_drop[:, m, :].unsqueeze(1), st[1], a_node[:, m, HEADS:].unsqueeze(1),
                                    ALU.subtract).then_inc(sa["m"], 1)
                if q.live(0):
                    dve.wait_ge(sa["e"], q.at(0, 4, 3))
                    V.tensor_scalar(a_e[:, e, :, :], a_l[:, e, :, :], 0.0, None, ALU.min
                                    ).then_inc(sa["e"], 1)
                if q.live(1):
                    dve.wait_ge(sa["part"], q.at(1, 4, 2))
                    V.tensor_scalar(a_part[:, m, 1, :], a_left[:, m, :], 1.0, None, ALU.mult
                                    ).then_inc(sa["part"], 1)
                if q.live(3):
                    hide(3).then_inc(sa["hide"], 1)
                if q.live(1):
                    dve.wait_ge(sa["m"], q.at(1, 5, 4))
                    V.tensor_scalar(st[1], a_node[:, m, HEADS:].unsqueeze(1), 1.0, None, ALU.mult
                                    ).then_inc(sa["m"], 1)
                if q.live(1):
                    dve.wait_ge(sa["part"], q.at(1, 4, 3))
                    V.tensor_tensor(a_part[:, m, 2, :], a_left[:, m, :], a_part[:, m, 1, :], ALU.subtract
                                    ).then_inc(sa["part"], 1)
                if q.live(-1):
                    j = q.slot(-1)
                    dve.wait_ge(sa["p"], q.at(-1, 1, 1))
                    V.tensor_tensor(
                        a_msg[:, j, :, :].rearrange("p t (h c) -> p t h c", h=HEADS),
                        a_rows[:, j, :, 0:ROW - HEADS].rearrange("p t (h c) -> p t h c", h=HEADS),
                        spread(a_p[:, j, :, :].unsqueeze(3), [P, T, HEADS, HC + 1]), ALU.mult
                    ).then_inc(sa["msg"], 1)
                if q.live(-2):
                    j = q.slot(-2)
                    b2 = dve.value_load(gat_block[0:1, bass.ds(q.at(-2), 1)], min_val=0, max_val=NB - 1)
                    dve.wait_ge(sa["scale"], q.at(-2, 1, 1))
                    dve.wait_ge(sa["pv"], q.at(-2, 1, 1))
                    dve.wait_ge(sa["add"], q.at(-2, 1, 1))
                    for h in range(HEADS):
                        hs = slice(h * (HC + 1), (h + 1) * (HC + 1))
                        part = acc[:, bass.ds(b2, 1), hs]
                        last = V.scalar_tensor_tensor(part, part, a_scale[:, j, h:h + 1],
                                                      bank[j % 3][:, hs].unsqueeze(1), ALU.mult, ALU.add)
                    last.then_inc(sa["add"], 1)
            run_steps(dve, GAT, 2, 4, body)
            dve.wait_ge(sa["add"], GAT.steps + 1)

            den = z[:, :, 0:HEADS]
            chain(V.tensor_scalar(den, acc_v[:, :, :, HC], 1e-16, None, ALU.add))
            chain(V.reciprocal(den, den))
            for h in range(HEADS):
                chain(V.tensor_tensor(acc_v[:, :, h, 0:HC], acc_v[:, :, h, 0:HC],
                                      spread(z[:, :, h:h + 1], [P, NB, HC]), ALU.mult))
            for h in range(HEADS):
                chain(V.tensor_tensor(acc_v[:, :, h, 0:HC], acc_v[:, :, h, 0:HC],
                                      spread(bias[:, 3, h * HC:(h + 1) * HC].unsqueeze(1), [P, NB, HC]),
                                      ALU.add))
            for h in range(HEADS):
                hs = slice(h * HC, (h + 1) * HC)
                chain(V.tensor_tensor(xs[:, :, hs], xs[:, :, hs], acc_v[:, :, h, 0:HC], ALU.add))
            layernorm(xs, 2)
            dve.sem_inc(s_fin, 1)


_INS = ["x", "src", "dst", "edge_type_4", "edge_weight", "L0_gnn_W1", "L0_gnn_b1", "L0_gnn_W2",
        "L0_gnn_b2", "L0_gnn_W3", "L0_gnn_b3", "L1_gnn_W", "L1_gnn_att_src", "L1_gnn_att_dst",
        "L1_gnn_bias"]


def kernel(**inputs):
    import numpy as _np
    import concourse.bacc as _bacc
    from concourse import mybir as _mybir
    from concourse.bass_utils import run_bass_kernel_spmd as _run

    nc = _bacc.Bacc("TRN2", target_bir_lowering=False, num_devices=1)
    arrays, args = {}, []
    for name in _INS:
        a = _np.ascontiguousarray(inputs[name])
        arrays[f"in_{name}"] = a
        args.append(nc.dram_tensor(f"in_{name}", a.shape, _mybir.dt.from_np(a.dtype),
                                   kind="ExternalInput").ap())
    out = nc.dram_tensor("out_x", (N_NODES, D), F32, kind="ExternalOutput").ap()
    gnn_kernel(nc, *args, out)
    r = _run(nc, [arrays], core_ids=[0])
    return r.results[0]["out_x"]
```

```python
from contextlib import ExitStack

import concourse.bass as bass
from concourse import mybir

F32, BF16 = mybir.dt.float32, mybir.dt.bfloat16
I32, U32, U8 = mybir.dt.int32, mybir.dt.uint32, mybir.dt.uint8
ALU = mybir.AluOpType
ACT = mybir.ActivationFunctionType
AX = mybir.AxisListType

P = 128
N_NODES, D, N_EDGES, N_TYPES, HEADS = 6250, 128, 206250, 4, 2
HC = D // HEADS
NB = -(-N_NODES // P)
FULL, REST = N_NODES // P, N_NODES % P
PAD_NODE = NB * P
NBINS = NB + 1
COLS = -(-N_EDGES // P)
LAST_COLS = N_EDGES - (P - 1) * COLS
SCATTER = 31
TURN = 2 * SCATTER
EARLY = (1, 4)
ACT_BINS = 29
HIST = 13
EDGES_PAD = P * COLS
BIG = 2.0 ** 100
NO_NODE = -1.0


class Plan:

    def __init__(self, tiles, part, ring):
        self.tiles, self.part, self.ring = tiles, part, ring
        per = tiles * P
        most = (N_EDGES + NB * (per - 1)) // per
        self.steps = -(-most // part)
        self.groups = self.steps * part
        self.step_tiles = tiles * part
        self.slots = max(self.groups * tiles, (most + 1) * tiles)
        self.shift = per.bit_length() - 1


GCN = Plan(tiles=1, part=10, ring=3)
GAT = Plan(tiles=4, part=1, ring=6)
ROW = HEADS * (HC + 1) + HEADS
GAT_W = ROW + HEADS
C = 7
CHUNKS = [slice(c * C, (c + 1) * C) for c in range(NB // C)]


class Step:

    def __init__(self, plan, base, i=None):
        self.plan, self.base, self.i = plan, base, i

    def live(self, lag):
        return self.i is not None or 0 <= self.base + lag < self.plan.steps

    def slot(self, lag):
        return (self.base + lag) % self.plan.ring

    def at(self, lag, times=1, plus=0):
        c = (self.base + lag) * times + plus
        return c if self.i is None else self.i * (self.plan.ring * times) + c

    def landed(self, lag, earlier=0, dmas=1):
        c = 16 * dmas * ((self.base + lag) // self.plan.ring + 1 + earlier)
        return c if self.i is None else self.i * (16 * dmas) + c


def run_steps(eng, plan, behind, ahead, body):
    whole = (plan.steps - ahead - behind) // plan.ring
    start, end = behind, behind + whole * plan.ring
    for q in range(-ahead, start):
        body(Step(plan, q))
    with eng.Fori(0, whole) as i:
        for j in range(plan.ring):
            body(Step(plan, start + j, i))
    for q in range(end, plan.steps + behind):
        body(Step(plan, q))


def wait_apart(eng, sem, value, count):
    eng.wait_ge(sem, value)
    eng.sem_inc(count, 1)


class Chain:

    def __init__(self, eng, sem):
        self.eng, self.sem, self.n = eng, sem, 0

    def __call__(self, ins):
        ins.then_inc(self.sem, 1)
        self.n += 1
        self.eng.wait_ge(self.sem, self.n)

    def loose(self, ins):
        ins.then_inc(self.sem, 1)
        self.n += 1
        self.eng.wait_ge(self.sem, self.n - 1)


def gnn_kernel(nc, x, src, dst, etype, weight, w1, b1, w2, b2, w3, b3, w_gat, att_src, att_dst,
               bias_gat, out):
    ctx = ExitStack()
    with ctx:
        def sb(name, shape, dt=F32, scope=ctx):
            return scope.enter_context(nc.sbuf_tensor(name, shape, dt))

        def sem(name):
            return ctx.enter_context(nc.semaphore(name))

        gcn_slots = nc.dram_tensor("gcn_slots", [P * GCN.slots, 3], F32).ap()
        by_dst = [nc.dram_tensor(f"by_dst_{n}", [EDGES_PAD + GAT.tiles * P, 1], dt).ap()
                  for n, dt in (("src", I32), ("dst", F32))]
        gcn_table = nc.dram_tensor("gcn_table", [NB * P * N_TYPES, D], F32).ap()
        gat_table = nc.dram_tensor("gat_table", [NB * P + 1, ROW], F32).ap()

        iota = sb("iota", [P, P])
        iota_b = sb("iota_b", [P, P], BF16)
        ident = sb("ident", [P, P])
        before = sb("before", [P, P])
        ones = sb("ones", [P, P])
        zeros = sb("zeros", [P, COLS], BF16)
        w_all = sb("w_all", [P, 3, N_TYPES * D])
        w_att = sb("w_att", [P, D])
        w_row = sb("w_row", [P, GAT_W])
        pad_row = sb("pad_row", [1, ROW])
        att_tmp = sb("att_tmp", [P, 2, D])
        bias = sb("bias", [P, 4, D])
        att = sb("att", [P, 2, D])
        inv_deg = sb("inv_deg", [P, NB])
        deg_mask = sb("deg_mask", [P, NB])
        falls_i = sb("falls_i", [1, 1], I32)
        gcn_block = sb("gcn_block", [1, GCN.groups], I32)
        gat_block = sb("gat_block", [1, GAT.groups], I32)
        gat_edge = sb("gat_edge", [1, GAT.groups], I32)
        gat_base = sb("gat_base", [P, GAT.groups])
        gcn_rec = sb("gcn_rec", [P, GCN.slots, 3])
        xs = sb("xs", [P, NB, D])
        stats = sb("stats", [P, NB, 6])
        mv = sb("mv", [P, NB, 2])
        nodeT = sb("nodeT", [P, 2, P])
        rows = sb("rows", [P, 4, N_TYPES * D])

        sort = ExitStack()
        src_i = sb("src_i", [P, COLS], I32, sort)
        dst_i = sb("dst_i", [P, COLS], I32, sort)
        type_i = sb("type_i", [P, COLS], I32, sort)
        tmp_i = sb("tmp_i", [P, COLS], I32, sort)
        w_f = sb("w_f", [P, COLS], F32, sort)
        block_of = [sb(f"block_of{s}", [P, COLS], F32, sort) for s in range(2)]
        dst_lo = sb("dst_lo", [P, COLS], F32, sort)
        mask = sb("mask", [P, COLS], U8, sort)
        rank = sb("rank", [P, COLS], F32, sort)
        place = w_f
        place_u = [sb(f"place_u{s}", [P, COLS], U32, sort) for s in range(2)]
        gcn_src = sb("gcn_src", [P, COLS, 3], F32, sort)
        at_stage = [sb(f"at_stage{h}", [P, SCATTER], U32, sort) for h in range(2)]
        rec_stage = [sb(f"rec_stage{h}", [P, SCATTER * 3], F32, sort) for h in range(2)]
        dst_f = rank
        pair_stage = [sb(f"pair_stage{n}", [P, SCATTER], dt, sort)
                      for n, dt in (("src", I32), ("dst", F32))]
        dst_next = sb("dst_next", [P, 1], I32, sort)
        pads = [sb(f"pads{n}", [P, GAT.tiles], dt, sort) for n, dt in (("src", I32), ("dst", F32))]
        falls = sb("falls", [P, 4], F32, sort)
        lo_hot = sb("lo_hot", [P, 2, HIST, P], BF16, sort)
        hi_hot = sb("hi_hot", [P, 2, HIST, NB], BF16, sort)
        bins = sb("bins", [P, 8, NBINS], F32, sort)
        below = sb("below", [P, ACT_BINS + 2], F32, sort)
        bins_i = sb("bins_i", [P, NBINS], I32, sort)
        start_col = sb("start_col", [NB, 2], F32, sort)
        passed = sb("passed", [NB, GCN.groups], F32, sort)
        iota_n = sb("iota_n", [P, GCN.groups], F32, sort)
        sort.close()

        acc = sb("acc", [P, NB, GAT_W])
        z = sb("z", [P, NB, D])
        gcn_scope = ExitStack()
        g_idx = sb("g_idx", [P, GCN.ring, GCN.step_tiles], U32, gcn_scope)
        g_lw = sb("g_lw", [P, GCN.ring, GCN.step_tiles, 2], F32, gcn_scope)
        g_rows = sb("g_rows", [P, GCN.ring, GCN.step_tiles, D], F32, gcn_scope)
        g_hot = sb("g_hot", [P, GCN.ring, GCN.step_tiles, P], F32, gcn_scope)
        gcn_scope.close()
        T, R = GAT.tiles, GAT.ring
        a_edge = [sb("a_src", [P, R, T], I32), sb("a_dst", [P, R, T])]
        a_lo = sb("a_lo", [P, R, T])
        a_rows = sb("a_rows", [P, R, T, ROW])
        a_miss = sb("a_miss", [P, R, T, P], BF16)
        a_hot = sb("a_hot", [P, R, T, P])
        a_cand = sb("a_cand", [P, 2, HEADS, T, P])
        a_hotT = sb("a_hotT", [P, R, T, P], BF16)
        a_msg = sb("a_msg", [P, R, T, HEADS * (HC + 1)])
        a_max = sb("a_max", [P, R, HEADS])
        a_sum = sb("a_sum", [P, R, HEADS])
        a_top = sb("a_top", [P, R, HEADS])
        a_part = sb("a_part", [P, R, 3, 2 * HEADS], BF16)
        a_left = sb("a_left", [P, R, 2 * HEADS])
        a_drop = sb("a_drop", [P, R, HEADS])
        a_scale = sb("a_scale", [P, R, HEADS])
        a_z = sb("a_z", [P, R, T, HEADS])
        a_l = sb("a_l", [P, R, T, HEADS])
        a_p = sb("a_p", [P, R, T, HEADS])
        state = sb("state", [P, NB, 3, HEADS])

        bank = [ctx.enter_context(nc.psum_tensor(f"bank{k}", [P, 512], F32)) for k in range(4)]
        wide = ctx.enter_context(nc.psum_tensor("wide", [P, 2, HEADS, T, P], F32))
        bank += [wide[:, k // 2, k % 2, :, :].rearrange("p t e -> p (t e)") for k in range(4)]

        s_const, s_fill, s_chain = sem("s_const"), sem("s_fill"), sem("s_chain")
        s_in = {n: sem(f"s_in_{n}") for n in ("src", "dst", "type", "weight", "x", "w", "bias", "att", "next")}
        s_empty = sem("s_empty")
        s_key, s_below = sem("s_key"), sem("s_below")
        s_seed, s_recs_load = sem("s_seed"), sem("s_recs_load")
        s_pre = sem("s_pre")
        s_pfx = sem("s_pfx")
        s_scol, s_scol2 = sem("s_scol"), sem("s_scol2")
        s_pass, s_pass2 = sem("s_pass"), sem("s_pass2")
        s_place = sem("s_place")
        s_stg = [sem(f"s_stg{h}") for h in range(2)]
        s_sct = [sem(f"s_sct{h}") for h in range(2)]
        s_pair, s_pair_stage, s_paired = sem("s_pair"), sem("s_pair_stage"), sem("s_paired")
        s_falls, s_falls2, s_falls3 = sem("s_falls"), sem("s_falls2"), sem("s_falls3")
        s_hot, s_cnt = sem("s_hot"), sem("s_cnt")
        s_sqrt = sem("s_sqrt")
        s_g = [sem(f"s_g{k}") for k in range(GCN.ring * GCN.step_tiles)]
        s_stage, s_ghot, s_gpe, s_gadd = ([sem(f"{n}{l}") for l in range(3)]
                                          for n in ("s_stage", "s_ghot", "s_gpe", "s_gadd"))
        s_z = [sem(f"s_z{l}") for l in range(4)]
        s_tT = [sem(f"s_tT{l}") for l in range(4)]
        s_tc = [sem(f"s_tc{l}") for l in range(4)]
        s_tm = [sem(f"s_tm{l}") for l in range(4)]
        s_tr = [sem(f"s_tr{l}") for l in range(4)]
        s_tw = [sem(f"s_tw{k}") for k in range(4)]
        s_ln, s_ln2 = sem("s_ln"), sem("s_ln2")
        s_row = sem("s_row")
        s_third, s_added = sem("s_third"), sem("s_added")
        s_den, s_scaled, s_summed = sem("s_den"), sem("s_scaled"), sem("s_summed")
        s_one = sem("s_one")
        s_gtw = sem("s_gtw")
        s_el = [sem(f"s_el{k}") for k in range(R)]
        sa = {n: sem(f"sa_{n}") for n in ("lo", "miss", "cand", "T", "hotT", "scale", "node", "p", "msg",
                                          "pv", "add", "max", "m1", "m2", "m3", "m4", "m5", "e1", "e2",
                                          "e3", "part1", "part2", "part3", "part4")}
        s_ag = [sem(f"s_ag{k}") for k in range(R)]
        s_apart = sem("s_apart")
        s_fin, s_out = sem("s_fin"), sem("s_out")

        cut = -(-GCN.groups // 4)
        begun_parts = [(bank[k][0:1, 0:min(cut, GCN.groups - n * cut)],
                        slice(n * cut, min((n + 1) * cut, GCN.groups)))
                       for n, k in enumerate((0, 5, 6, 7))]

        acc_v = acc[:, :, 0:HEADS * (HC + 1)].rearrange("p b (h c) -> p b h c", h=HEADS)

        def sum_of(g):
            return bank[g // 4][:, g % 4 * D:(g % 4 + 1) * D]

        def spread(ap, shape):
            return ap.to_broadcast(shape)

        block = ctx.enter_context(nc.Block())

        def tw_before(layer, k):
            return layer * len(range(k, NB, 4))

        @block.sync
        def _(sp):
            def load_edges(name, dram, tile):
                flat = dram.rearrange("(o n) -> o n", o=1)
                body = flat[0:1, 0:(P - 1) * COLS].rearrange("o (p c) -> (o p) c", p=P - 1)
                sp.dma_start(tile[0:P - 1, :], body).then_inc(s_in[name], 16)
                sp.dma_start(tile[P - 1:P, 0:LAST_COLS], flat[0:1, (P - 1) * COLS:]).then_inc(s_in[name], 16)

            sp.wait_ge(s_fill, 4)
            load_edges("src", src, src_i)
            load_edges("dst", dst, dst_i)
            load_edges("type", etype, type_i)
            load_edges("weight", weight, w_f)
            sp.wait_ge(s_fill, 5)
            sp.dma_start(xs[:, 0:FULL, :],
                         x[0:FULL * P, :].rearrange("(b p) f -> p b f", p=P)).then_inc(s_in["x"], 16)
            sp.dma_start(xs[0:REST, FULL, :], x[FULL * P:, :]).then_inc(s_in["x"], 16)
            for l, w in enumerate((w1, w2, w3)):
                sp.dma_start(w_all[:, l, :].rearrange("i (t o) -> i t o", t=N_TYPES),
                             w.rearrange("t i o -> i t o")).then_inc(s_in["w"], 16)
            sp.dma_start(w_att[:, :], w_gat).then_inc(s_in["w"], 16)
            for l, b in enumerate((b1, b2, b3, bias_gat)):
                sp.dma_start(bias[:, l, :], b.partition_broadcast(P)).then_inc(s_in["bias"], 16)
            for l, a in enumerate((att_src, att_dst)):
                sp.dma_start(att[:, l, :], a.rearrange("h c -> (h c)").partition_broadcast(P)
                             ).then_inc(s_in["att"], 16)
            sp.wait_ge(s_fill, 8)
            sp.dma_start(dst_next[0:P - 1, :],
                         dst[COLS:].rearrange("(n o) -> n o", o=1)[0:(P - 2) * COLS + 1:COLS, :],
                         allow_slow_non_contiguous=True).then_inc(s_in["next"], 16)
            sp.wait_ge(s_empty, 2)
            sp.dma_start(gcn_slots.rearrange("(p t) k -> p (t k)", p=P),
                         gcn_rec[:, :, :].rearrange("p t k -> p (t k)")).then_inc(s_seed, 16)
            for n in range(2):
                sp.dma_start(by_dst[n][EDGES_PAD:, 0].rearrange("(p t) -> p t", p=P), pads[n][:, :]
                             ).then_inc(s_seed, 16)

            def write_table(layer, table):
                for b in range(NB):
                    k = b % 4
                    sp.wait_ge(s_tr[layer], b + 1)
                    width = table.shape[1]
                    sp.dma_start(table[b * P:(b + 1) * P, :],
                                 rows[:, k, 0:width]).then_inc(s_tw[k], 16)

            gcn_wide = gcn_table.rearrange("(n t) f -> n (t f)", t=N_TYPES)
            write_table(0, gcn_wide)
            for h in range(2):
                sp.wait_ge(s_sct[h], 16 * SCATTER * (COLS // TURN))
            sp.dma_start(gcn_rec[:, :, :].rearrange("p t k -> p (t k)"),
                         gcn_slots.rearrange("(p t) k -> p (t k)", p=P)).then_inc(s_recs_load, 16)
            write_table(1, gcn_wide)
            write_table(2, gcn_wide)
            sp.wait_ge(s_row, 1)
            sp.dma_start(gat_table[NB * P:, :], pad_row[:, :]).then_inc(s_gtw, 16)
            for c, cs in enumerate(CHUNKS):
                sp.wait_ge(s_one, c + 1)
                sp.dma_start(gat_table[0:NB * P, :].rearrange("(b p) w -> p b w", p=P)[:, cs, :], acc[:, cs, 0:ROW]
                             ).then_inc(s_gtw, 16)
            sp.wait_ge(s_paired, 1)

            def body(q):
                if not q.live(0):
                    return
                e = sp.value_load(gat_edge[0:1, bass.ds(q.at(0), 1)], min_val=0, max_val=EDGES_PAD)
                if q.live(-R):
                    wait_apart(sp, sa["cand"], q.at(-R, 1, 1), s_apart)
                for n in range(2):
                    sp.dma_start(a_edge[n][:, q.slot(0), :],
                                 by_dst[n][bass.ds(e, T * P), 0].rearrange("(p t) -> p t", p=P)
                                 ).then_inc(s_el[q.slot(0)], 16)
            run_steps(sp, GAT, R, 0, body)
            for c, cs in enumerate(CHUNKS):
                sp.wait_ge(s_fin, c + 1)
                full = min(cs.stop, FULL)
                sp.dma_start(out[cs.start * P:full * P, :].rearrange("(b p) f -> p b f", p=P),
                             xs[:, cs.start:full, :]).then_inc(s_out, 16)
            sp.dma_start(out[FULL * P:, :], xs[0:REST, FULL, :]).then_inc(s_out, 16)
            sp.wait_ge(s_out, 16 * (len(CHUNKS) + 1))

        @block.gpsimd
        def _(pool):
            nc.gpsimd.iota(iota[:, :], [[1, P]], base=0, channel_multiplier=0,
                           allow_small_or_imprecise_dtypes=True)
            nc.gpsimd.iota(iota_b[:, :], [[1, P]], base=0, channel_multiplier=0,
                           allow_small_or_imprecise_dtypes=True)
            nc.gpsimd.iota(iota_n[:, :], [[1, GCN.groups]], base=0, channel_multiplier=0,
                           allow_small_or_imprecise_dtypes=True)
            nc.gpsimd.memset(ones[:, :], 1.0).then_inc(s_const, 1)
            pool.wait_ge(s_const, 1)
            nc.gpsimd.affine_select(out=ident[:, :], in_=ones[:, :], compare_op=ALU.is_equal, fill=0.0,
                                    base=0, pattern=[[1, P]], channel_multiplier=-1)
            nc.gpsimd.affine_select(out=before[:, :], in_=ones[:, :], compare_op=ALU.is_gt, fill=0.0,
                                    base=0, pattern=[[1, P]], channel_multiplier=-1).then_inc(s_const, 1)
            nc.gpsimd.memset(gcn_rec[:, :, :], 0.0).then_inc(s_empty, 1)
            pool.wait_ge(s_empty, 1)
            nc.gpsimd.memset(gcn_rec[:, :, 1:2], NO_NODE).then_inc(s_empty, 1)
            pool.wait_ge(s_seed, 48)
            with pool.Fori(0, COLS // TURN) as i:
                for h in range(2):
                    wait_apart(pool, s_stg[h], i * 2 + 2, s_apart)
                    for c in range(SCATTER):
                        pool.indirect_dma_start(
                            out=gcn_slots, out_offset=bass.IndirectOffsetOnAxis(
                                ap=at_stage[h][:, c:c + 1], axis=0),
                            in_=rec_stage[h][:, c * 3:(c + 1) * 3], in_offset=None,
                        ).then_inc(s_sct[h], 16)

            pool.wait_ge(s_falls3, 1)
            pool.wait_ge(s_place, len(EARLY) + 2)
            for h in range(2):
                pool.wait_ge(s_sct[h], 16 * SCATTER * (COLS // TURN))
            fell = pool.value_load(falls_i[0:1, 0:1], min_val=0, max_val=P)
            with pool.If(fell < 1):
                for n, tile in enumerate((src_i, dst_f)):
                    pool.dma_start(by_dst[n][0:EDGES_PAD, 0].rearrange("(p c) -> p c", p=P), tile[:, :]
                                   ).then_inc(s_pair, 16)
                pool.wait_ge(s_pair, 32)
            with pool.Else():
                with pool.Fori(0, COLS // SCATTER) as i:
                    at = bass.ds(i * SCATTER, SCATTER)
                    pool.tensor_copy(at_stage[0][:, :], place_u[1][:, at]).then_inc(s_pair_stage, 1)
                    for n, tile in enumerate((src_i, dst_f)):
                        pool.tensor_copy(pair_stage[n][:, :], tile[:, at]).then_inc(s_pair_stage, 1)
                    wait_apart(pool, s_pair_stage, i * 3 + 3, s_apart)
                    for n in range(2):
                        for c in range(SCATTER):
                            pool.indirect_dma_start(
                                out=by_dst[n], out_offset=bass.IndirectOffsetOnAxis(
                                    ap=at_stage[0][:, c:c + 1], axis=0),
                                in_=pair_stage[n][:, c:c + 1], in_offset=None,
                            ).then_inc(s_pair, 16)
                    wait_apart(pool, s_pair, i * (32 * SCATTER) + 32 * SCATTER, s_apart)
            pool.sem_inc(s_paired, 1)

            def gather_gcn(layer):
                for k in range(4):
                    pool.wait_ge(s_tw[k], 16 * tw_before(layer + 1, k))

                def body(q):
                    wait_apart(pool, s_stage[layer], q.at(0, 2, 2), s_apart)
                    for t in range(GCN.step_tiles):
                        pool.indirect_dma_start(
                            out=g_rows[:, q.slot(0), t, :], out_offset=None, in_=gcn_table,
                            in_offset=bass.IndirectOffsetOnAxis(
                                ap=g_idx[:, q.slot(0), t:t + 1], axis=0),
                        ).then_inc(s_g[q.slot(0) * GCN.step_tiles + t], 16)
                run_steps(pool, GCN, 0, 0, body)

            for layer in range(3):
                gather_gcn(layer)

            for c in range(len(CHUNKS) + 3):
                if c < len(CHUNKS):
                    cs = CHUNKS[c]
                    pool.wait_ge(s_third, c + 1)
                    nc.gpsimd.tensor_tensor(xs[:, cs, :], xs[:, cs, :], z[:, cs, :], ALU.add
                                            ).then_inc(s_added, 1)
                if c >= 3:
                    pool.wait_ge(s_tr[3], (c - 2) * C)
                    nc.gpsimd.memset(acc_v[:, CHUNKS[c - 3], :, HC:], 1.0).then_inc(s_one, 1)
            pool.wait_ge(s_gtw, 16 * (len(CHUNKS) + 1))

            def body(q):
                if not q.live(0):
                    return
                if q.live(-R):
                    wait_apart(pool, sa["msg"], q.at(-R, 1, 1), s_apart)
                wait_apart(pool, s_el[q.slot(0)], q.landed(0, 0, 2), s_apart)
                for t in range(T):
                    pool.indirect_dma_start(
                        out=a_rows[:, q.slot(0), t, :], out_offset=None, in_=gat_table,
                        in_offset=bass.IndirectOffsetOnAxis(ap=a_edge[0][:, q.slot(0), t:t + 1].bitcast(U32), axis=0),
                    ).then_inc(s_ag[q.slot(0)], 16)
            run_steps(pool, GAT, R, 0, body)

            pool.wait_ge(s_den, 1)
            for c, cs in enumerate(CHUNKS):
                part = acc_v[:, cs, :, 0:HC]
                xs_v = xs[:, cs, :].rearrange("p b (h c) -> p b h c", h=HEADS)
                nc.gpsimd.tensor_tensor(part, part, spread(z[:, cs, 0:HEADS].unsqueeze(3), [P, C, HEADS, HC]),
                                        ALU.mult).then_inc(s_scaled, 1)
                pool.wait_ge(s_scaled, c + 1)
                nc.gpsimd.tensor_tensor(xs_v, xs_v, part, ALU.add).then_inc(s_summed, 1)

        @block.scalar
        def _(act):
            act.wait_ge(s_const, 2)
            act.wait_ge(s_key, 1)
            unread = lo_hot[:, :, :, :].rearrange("p h c n -> p h (c n)")
            for n, b in enumerate(range(1, ACT_BINS + 1)):
                if n >= 2:
                    act.wait_ge(s_below, n - 1)
                nc.scalar.activation(unread[:, n % 2, 0:COLS], block_of[0][:, :], ACT.Relu,
                                     bias=iota[:, b:b + 1], scale=-1.0,
                                     accum_out=below[:, b + 1:b + 2]).then_inc(s_below, 1)
            act.wait_ge(s_place, 1)

            def stage(i, h):
                col = i * TURN + h * SCATTER
                nc.scalar.copy(at_stage[h][:, :], place_u[0][:, bass.ds(col, SCATTER)]).then_inc(s_stg[h], 1)
                nc.scalar.copy(rec_stage[h][:, :].rearrange("p (c k) -> p c k", k=3),
                               gcn_src[:, bass.ds(col, SCATTER), :]).then_inc(s_stg[h], 1)
            for h in range(2):
                stage(0, h)
            turns = COLS // TURN
            middle = turns // 2
            runs = [(1, sum(EARLY), 2), (sum(EARLY), middle, len(EARLY) + 1), (middle, turns, 0)]
            for first, end, places in runs:
                if places:
                    act.wait_ge(s_place, places)
                with act.Fori(first, end) as i:
                    for h in range(2):
                        act.wait_ge(s_sct[h], i * (16 * SCATTER))
                        stage(i, h)
                if end == middle:
                    act.wait_ge(s_sqrt, 1)
                    nc.scalar.sqrt(inv_deg[:, :], inv_deg[:, :]).then_inc(s_sqrt, 1)

            def table(layer):
                for b in range(NB):
                    act.wait_ge(s_tT[layer], b + 1)
                    nc.scalar.copy(nodeT[:, b % 2, :], bank[4 + b % 2][:, 0:P]
                                   ).then_inc(s_tc[layer], 1)
                    if b >= 1:
                        row(layer, b - 1)
                row(layer, NB - 1)

            def row(layer, b):
                act.wait_ge(s_tm[layer], b + 1)
                if b >= 4 or layer:
                    act.wait_ge(s_tw[b % 4], 16 * (tw_before(layer, b % 4) + b // 4))
                nc.scalar.activation(rows[:, b % 4, :], bank[2 + b % 2][:, :], ACT.Copy,
                                     scale=inv_deg[:, b:b + 1]).then_inc(s_tr[layer], 1)
            table(1)
            table(2)

            def ln_sqrt(n):
                cs = CHUNKS[n % len(CHUNKS)]
                act.wait_ge(s_ln, n + 1)
                nc.scalar.sqrt(mv[:, cs, 1], mv[:, cs, 1]).then_inc(s_ln2, 1)

            def gat_row(b):
                act.wait_ge(s_tm[3], b + 1)
                nc.scalar.copy(acc[:, b, :], bank[2 + b % 2][:, 0:GAT_W]).then_inc(s_tr[3], 1)

            for c in range(len(CHUNKS) + 2):
                if c < len(CHUNKS):
                    ln_sqrt(c)
                if c >= 2:
                    chunk = range((c - 2) * C, (c - 1) * C)
                    for b in chunk:
                        act.wait_ge(s_tT[3], b + 1)
                        nc.scalar.copy(nodeT[:, b % 2, :], bank[4 + b % 2][:, 0:P]
                                       ).then_inc(s_tc[3], 1)
                        if b > chunk.start:
                            gat_row(b - 1)
                    gat_row(chunk.stop - 1)

            def body(q):
                if q.live(1):
                    act.wait_ge(sa["max"], q.at(1, 1, 1))
                    nc.scalar.activation(a_hotT[:, q.slot(1), :, :], wide[:, q.slot(1) % 2, 0, :, :],
                                         ACT.Identity, bias=1.0, scale=1.0 / BIG).then_inc(sa["hotT"], 1)
                if q.live(3):
                    j, w = q.slot(3), q.slot(3) % 2
                    act.wait_ge(sa["miss"], q.at(3, 1, 1))
                    nc.scalar.activation(a_hot[:, j, :, :], a_miss[:, j, :, :], ACT.Identity,
                                         bias=1.0, scale=-1.0)
                    if q.live(1):
                        act.wait_ge(sa["T"], q.at(1, 1, 1))
                    act.wait_ge(s_ag[j], q.landed(3, 0, T))
                    for t in range(T):
                        for h in range(HEADS):
                            last = nc.scalar.activation(
                                a_cand[:, w, h, t, :], a_miss[:, j, t, :], ACT.Identity, scale=-BIG,
                                bias=a_rows[:, j, t, ROW - HEADS + h:ROW - HEADS + h + 1])
                    last.then_inc(sa["cand"], 1)
                if q.live(1):
                    act.wait_ge(sa["m4"], q.at(1, 1, 1))
                    nc.scalar.activation(a_scale[:, q.slot(1), :], a_drop[:, q.slot(1), :], ACT.Exp
                                         ).then_inc(sa["scale"], 1)
                if q.live(0):
                    act.wait_ge(sa["e3"], q.at(0, 1, 1))
                    nc.scalar.activation(a_p[:, q.slot(0), :, :], a_l[:, q.slot(0), :, :], ACT.Exp
                                         ).then_inc(sa["p"], 1)

            run_steps(act, GAT, 2, 4, body)
            for c in range(len(CHUNKS)):
                ln_sqrt(len(CHUNKS) + c)

        @block.tensor
        def _(pe):
            pe.wait_ge(s_const, 2)

            def ranks(s):
                pe.wait_ge(s_pre, s + 1)
                nc.tensor.matmul(bank[1][:, 0:NBINS], before[:, :], bins[:, 0, :], start=True, stop=True)
                nc.tensor.matmul(bank[1][:, 64:64 + NBINS], ones[:, :], bins[:, 0, :],
                                 start=True, stop=True).then_inc(s_pfx, 1)
                pe.wait_ge(s_scol, s + 1)
                for n, row in enumerate((4, 7)[:s + 1]):
                    last = nc.tensor.matmul(bank[0][0:NB, 500 + n:501 + n], bins[0:1, row, 0:NB],
                                            ones[0:1, 0:1], start=True, stop=True)
                last.then_inc(s_scol2, 1)
                pe.wait_ge(s_pass, s + 1)
                if s == 0:
                    for ps, at in begun_parts:
                        last = nc.tensor.matmul(ps, ones[0:NB, 0:1], passed[:, at], start=True, stop=True)
                    last.then_inc(s_pass2, 1)
                else:
                    nc.tensor.matmul(bank[0][:, 0:GAT.groups], ones[0:NB, :], passed[:, 0:GAT.groups],
                                     start=True, stop=True)
                    nc.tensor.matmul(bank[5][0:1, 0:GAT.groups], start_col[:, 1:2], passed[:, 0:GAT.groups],
                                     start=True, stop=True).then_inc(s_pass2, 1)

            ranks(0)
            pe.wait_ge(s_hot, 1)
            nc.tensor.matmul(bank[1][:, 256:256 + NB], lo_hot[:, 0, 0, :], zeros[:, 0:NB],
                             start=True, stop=False).then_inc(s_cnt, 1)
            with pe.Fori(0, COLS // (2 * HIST)) as i:
                for h in range(2):
                    pe.wait_ge(s_hot, i * 2 + h + 1)
                    for c in range(HIST):
                        last = nc.tensor.matmul(bank[1][:, 256:256 + NB], lo_hot[:, h, c, :],
                                                hi_hot[:, h, c, :], start=False, stop=False,
)
                    last.then_inc(s_cnt, 1)
            nc.tensor.matmul(bank[1][:, 256:256 + NB], lo_hot[:, 0, 0, :], zeros[:, 0:NB],
                             start=False, stop=True).then_inc(s_cnt, 1)

            def table(layer, node, w):
                def product(b):
                    pe.wait_ge(s_tc[layer], b + 1)
                    if b >= 2:
                        pe.wait_ge(s_tr[layer], b - 1)
                    nc.tensor.matmul(bank[2 + b % 2][:, 0:w.shape[1]], nodeT[:, b % 2, :], w,
                                     start=True, stop=True).then_inc(s_tm[layer], 1)
                for b in range(NB):
                    pe.wait_ge(s_z[layer], b + 1 if layer else 1)
                    if b >= 2:
                        pe.wait_ge(s_tc[layer], b - 1)
                    nc.tensor.transpose(bank[4 + b % 2][:, 0:P], node[:, b, :], ident[:, :]
                                        ).then_inc(s_tT[layer], 1)
                    if b >= 1:
                        product(b - 1)
                product(NB - 1)

            pe.wait_ge(s_in["x"], 32)
            pe.wait_ge(s_in["w"], 64)
            table(0, xs, w_all[:, 0, :])
            ranks(1)
            pe.wait_ge(s_falls, 1)
            nc.tensor.matmul(bank[3][0:1, 0:1], falls[:, 3:4], ones[:, 0:1], start=True, stop=True
                             ).then_inc(s_falls2, 1)

            def sum_gcn(layer):
                def body(q):
                    j = q.slot(0)
                    pe.wait_ge(s_ghot[layer], q.at(0, 1, 1))
                    pe.wait_ge(s_gadd[layer], q.at(0, GCN.part, 1))
                    for g in range(GCN.part):
                        for t in range(GCN.tiles):
                            k = g * GCN.tiles + t
                            pe.wait_ge(s_g[j * GCN.step_tiles + k],
                                       q.landed(0, layer * len(range(j, GCN.steps, GCN.ring))))
                            last = nc.tensor.matmul(sum_of(g), g_hot[:, j, k, :], g_rows[:, j, k, :],
                                                    start=(t == 0), stop=(t == GCN.tiles - 1))
                        last.then_inc(s_gpe[layer], 1)
                run_steps(pe, GCN, 0, 0, body)

            sum_gcn(0)
            table(1, z, w_all[:, 1, :])
            sum_gcn(1)
            table(2, z, w_all[:, 2, :])
            sum_gcn(2)
            pe.wait_ge(s_row, 1)
            table(3, z, w_row[:, :])

            def body(q):
                if q.live(2):
                    j, w = q.slot(2), q.slot(2) % 2
                    pe.wait_ge(sa["cand"], q.at(2, 1, 1))
                    if q.live(0):
                        pe.wait_ge(sa["hotT"], q.at(0, 1, 1))
                    for h in range(HEADS):
                        for t in range(T):
                            last = nc.tensor.transpose(wide[:, w, h, t, :], a_cand[:, w, h, t, :],
                                                       ident[:, :])
                    last.then_inc(sa["T"], 1)
                if q.live(1):
                    j = q.slot(1)
                    pe.wait_ge(sa["part4"], q.at(1, 1, 1))
                    pe.wait_ge(sa["hotT"], q.at(1, 1, 1))
                    if q.live(0):
                        pe.wait_ge(sa["e3"], q.at(0, 1, 1))
                    for t in range(T):
                        for k in range(3):
                            last = nc.tensor.matmul(bank[3][:, t * 4:(t + 1) * 4], a_hotT[:, j, t, :],
                                                    a_part[:, j, k, :], start=(k == 0), stop=(k == 2))
                    last.then_inc(sa["node"], 1)
                if q.live(-1):
                    pe.wait_ge(sa["msg"], q.at(-1, 1, 1))
                    if q.live(-4):
                        pe.wait_ge(sa["add"], q.at(-4, 1, 2))
                    j = q.slot(-1)
                    for t in range(T):
                        last = nc.tensor.matmul(bank[j % 3][:, 0:HEADS * (HC + 1)], a_hot[:, j, t, :],
                                                a_msg[:, j, t, :], start=(t == 0), stop=(t == T - 1))
                    last.then_inc(sa["pv"], 1)
            run_steps(pe, GAT, 2, 4, body)

        @block.vector
        def _(dve):
            V = nc.vector
            chain = Chain(dve, s_chain)
            V.memset(src_i[:, LAST_COLS:], PAD_NODE).then_inc(s_fill, 1)
            V.memset(dst_i[:, LAST_COLS:], PAD_NODE).then_inc(s_fill, 1)
            V.memset(type_i[:, LAST_COLS:], 0).then_inc(s_fill, 1)
            V.memset(w_f[:, LAST_COLS:], 0.0).then_inc(s_fill, 1)
            V.memset(xs[:, FULL, :], 0.0).then_inc(s_fill, 1)
            V.memset(pads[0][:, :], PAD_NODE)
            V.memset(pads[1][:, :], float(PAD_NODE)).then_inc(s_fill, 1)
            V.memset(dst_next[:, :], PAD_NODE).then_inc(s_fill, 1)
            V.memset(below[:, 0:2], 0.0).then_inc(s_fill, 1)
            V.memset(zeros[:, :], 0.0).then_inc(s_fill, 1)

            def split(node_i, s, lo):
                chain(V.tensor_scalar(tmp_i[:, :], node_i[:, :], 7, None, ALU.logical_shift_right))
                chain(V.tensor_copy(block_of[s][:, :], tmp_i[:, :]))
                if s == 0:
                    dve.sem_inc(s_key, 1)
                chain(V.tensor_scalar(tmp_i[:, :], node_i[:, :], P - 1, None, ALU.bitwise_and))
                chain(V.tensor_scalar(rank[:, :], block_of[s][:, :], float(NB), -4.0 * P,
                                      ALU.is_equal, ALU.mult))
                chain(V.tensor_tensor(lo, tmp_i[:, :], rank[:, :], ALU.add))

            def early_ranks(key, cs):
                n = cs.stop - cs.start
                masks = [mask[:, k * n:(k + 1) * n] for k in range(3)]
                ranks = [rank[:, k * n:(k + 1) * n] for k in range(2)]
                for b in range(NBINS + 2):
                    if b < NBINS:
                        chain.loose(V.tensor_scalar(masks[b % 3], key[:, cs], float(b), None,
                                                    ALU.is_equal))
                    else:
                        dve.wait_ge(s_chain, chain.n)
                    if 0 <= b - 1 < NBINS:
                        chain.loose(V.tensor_tensor_scan(ranks[(b - 1) % 2], masks[(b - 1) % 3],
                                                         zeros[:, 0:n], bins[:, 6, b - 1:b],
                                                         ALU.add, ALU.add))
                    if b >= 2:
                        r = ranks[b % 2]
                        chain.loose(V.copy_predicated(place[:, cs], masks[(b - 2) % 3], r))
                        chain.loose(V.tensor_copy(bins[:, 6, b - 2:b - 1], r[:, n - 1:n]))
                dve.wait_ge(s_chain, chain.n)

            def slot_numbers(plan, cs):
                number = place_u[0][:, cs]
                chain(V.tensor_copy(number, place[:, cs]))
                chain(V.tensor_scalar(tmp_i[:, cs], number.bitcast(I32), 7, None, ALU.logical_shift_right))
                chain(V.tensor_copy(rank[:, cs], tmp_i[:, cs]))
                chain(V.tensor_scalar(tmp_i[:, cs], number.bitcast(I32), P - 1, None, ALU.bitwise_and))
                chain(V.tensor_copy(place[:, cs], tmp_i[:, cs]))
                chain(V.scalar_tensor_tensor(number, place[:, cs], float(plan.slots), rank[:, cs],
                                             ALU.mult, ALU.add))

            def places(s, plan):
                key = block_of[s]
                for b in range(0 if s else ACT_BINS, NBINS):
                    chain(V.tensor_scalar(mask[:, :], key[:, :], float(b), None, ALU.is_equal, ALU.add,
                                          accum_out=bins[:, 0, b:b + 1]))
                if s == 0:
                    dve.wait_ge(s_below, ACT_BINS)
                    lowest = bins[:, 0, 0:ACT_BINS]
                    chain(V.scalar_tensor_tensor(lowest, below[:, 1:ACT_BINS + 1], -2.0,
                                                 below[:, 0:ACT_BINS], ALU.mult, ALU.add))
                    chain(V.tensor_tensor(lowest, lowest, below[:, 2:], ALU.add))
                dve.sem_inc(s_pre, 1)
                dve.wait_ge(s_pfx, s + 1)
                per = plan.tiles * P
                lower, total = bank[1][:, 0:NBINS], bank[1][:, 64:64 + NBINS]
                chain(V.tensor_scalar(bins[:, 1, :], total, float(per - 1), None, ALU.add))
                chain(V.tensor_copy(bins_i[:, :], bins[:, 1, :]))
                chain(V.tensor_scalar(bins_i[:, :], bins_i[:, :], plan.shift, None, ALU.logical_shift_right))
                chain(V.tensor_copy(bins[:, 2, :], bins_i[:, :]))
                chain(V.tensor_tensor_scan(bins[:, 3, :], bins[:, 2, :], zeros[:, 0:NBINS], 0.0,
                                           ALU.add, ALU.add))
                chain(V.tensor_tensor(bins[:, 4, :], bins[:, 3, :], bins[:, 2, :], ALU.subtract))
                if s == 0:
                    chain(V.tensor_scalar(bins[:, 5, :], bins[:, 4, :], float(per), -1.0,
                                          ALU.mult, ALU.add))
                else:
                    chain(V.tensor_tensor_scan(bins[:, 3, :], total, zeros[:, 0:NBINS], -1.0,
                                               ALU.add, ALU.add))
                    chain(V.tensor_tensor(bins[:, 5, :], bins[:, 3, :], total, ALU.subtract))
                    chain(V.scalar_tensor_tensor(bins[:, 1, :], bins[:, 4, :], -float(per), bins[:, 5, :],
                                                 ALU.mult, ALU.add))
                    chain(V.tensor_scalar(bins[:, 1, :], bins[:, 1, :], 1.0, None, ALU.add))
                    chain(V.tensor_copy(bins[:, 7, 0:1], bins[:, 1, 0:1]))
                    chain(V.tensor_tensor(bins[:, 7, 1:], bins[:, 1, 1:], bins[:, 1, 0:NBINS - 1],
                                          ALU.subtract))
                dve.sem_inc(s_scol, 1)
                chain(V.tensor_tensor(bins[:, 6, :], bins[:, 5, :], lower, ALU.add))
                if s == 0:
                    for n, turns in enumerate(EARLY):
                        cs = slice(sum(EARLY[0:n]) * TURN, sum(EARLY[0:n + 1]) * TURN)
                        early_ranks(key, cs)
                        slot_numbers(plan, cs)
                        dve.sem_inc(s_place, 1)
                rest = slice(0 if s else sum(EARLY) * TURN, COLS)
                for b in range(NBINS):
                    chain(V.tensor_scalar(mask[:, rest], key[:, rest], float(b), None, ALU.is_equal))
                    chain(V.tensor_tensor_scan(rank[:, rest], mask[:, rest], zeros[:, rest],
                                               bins[:, 6, b:b + 1], ALU.add, ALU.add))
                    chain(V.copy_predicated(place[:, rest], mask[:, rest], rank[:, rest]))
                if s == 0:
                    slot_numbers(plan, rest)
                else:
                    chain(V.tensor_copy(place_u[s][:, :], place[:, :]))
                dve.sem_inc(s_place, 1)
                dve.wait_ge(s_scol2, s + 1)
                chain(V.tensor_copy(start_col[:, 0:s + 1], bank[0][0:NB, 500:501 + s]))
                chain(V.tensor_scalar(passed[:, :], iota_n[0:NB, :], start_col[:, 0:1], None, ALU.is_ge))
                dve.sem_inc(s_pass, 1)
                dve.wait_ge(s_pass2, s + 1)
                if s == 0:
                    for ps, at in begun_parts:
                        chain(V.tensor_scalar(gcn_block[:, at], ps, -1.0, None, ALU.add))
                else:
                    begun = bank[0][:, 0:GAT.groups]
                    chain(V.tensor_scalar(gat_block[:, :], begun[0:1, :], -1.0, None, ALU.add))
                    chain(V.tensor_scalar(gat_base[:, :], begun, float(P), -float(P), ALU.mult, ALU.add))
                    chain(V.scalar_tensor_tensor(passed[0:1, 0:GAT.groups], iota_n[0:1, 0:GAT.groups],
                                                 float(per), bank[5][0:1, 0:GAT.groups],
                                                 ALU.mult, ALU.add))
                    chain(V.tensor_scalar(gat_edge[:, :], passed[0:1, 0:GAT.groups], float(EDGES_PAD),
                                          None, ALU.min))

            dve.wait_ge(s_in["src"], 32)
            split(src_i, 0, gcn_src[:, :, 1])
            dve.wait_ge(s_in["dst"], 32)
            dve.wait_ge(s_in["type"], 32)
            dve.wait_ge(s_in["weight"], 32)
            chain(V.tensor_copy(gcn_src[:, :, 2], w_f[:, :]))
            chain(V.scalar_tensor_tensor(rank[:, :], dst_i[:, :], float(N_TYPES), type_i[:, :],
                                         ALU.mult, ALU.add))
            chain(V.tensor_scalar(gcn_src[:, :, 0], rank[:, :], float(NB * P * N_TYPES - 1), None, ALU.min))
            dve.wait_ge(s_const, 2)
            dve.wait_ge(s_fill, 9)
            places(0, GCN)
            split(dst_i, 1, dst_lo[:, :])

            def hots(i, h):
                col = i * (2 * HIST) + h * HIST
                lo = dst_lo[:, bass.ds(col, HIST)].unsqueeze(2)
                hi = block_of[1][:, bass.ds(col, HIST)].unsqueeze(2)
                V.tensor_tensor(lo_hot[:, h, :, :], spread(iota[:, :].unsqueeze(1), [P, HIST, P]),
                                spread(lo, [P, HIST, P]), ALU.is_equal)
                V.tensor_tensor(hi_hot[:, h, :, :], spread(iota[:, 0:NB].unsqueeze(1), [P, HIST, NB]),
                                spread(hi, [P, HIST, NB]), ALU.is_equal).then_inc(s_hot, 1)
            for h in range(2):
                hots(0, h)
            with dve.Fori(1, COLS // (2 * HIST)) as i:
                for h in range(2):
                    dve.wait_ge(s_cnt, i * 2 + h)
                    hots(i, h)
            dve.wait_ge(s_cnt, 2 * (COLS // (2 * HIST)) + 2)
            deg = bank[1][:, 256:256 + NB]
            chain(V.tensor_scalar(inv_deg[:, :], deg, 1.0, None, ALU.max))
            chain(V.tensor_scalar(deg_mask[:, :], deg, 0.0, None, ALU.is_gt))
            dve.sem_inc(s_sqrt, 1)
            dve.wait_ge(s_sqrt, 2)
            chain(V.reciprocal(inv_deg[:, :], inv_deg[:, :]))
            chain(V.tensor_tensor(inv_deg[:, :], inv_deg[:, :], deg_mask[:, :], ALU.mult))
            dve.sem_inc(s_z[0], 1)

            def row0(b):
                dve.wait_ge(s_tm[0], b + 1)
                if b >= 4:
                    dve.wait_ge(s_tw[b % 4], 16 * (b // 4))
                V.tensor_scalar(rows[:, b % 4, :], bank[2 + b % 2][:, :], inv_deg[:, b:b + 1], None,
                                ALU.mult).then_inc(s_tr[0], 1)
            for b in range(NB):
                dve.wait_ge(s_tT[0], b + 1)
                V.tensor_copy(nodeT[:, b % 2, :], bank[4 + b % 2][:, 0:P]
                              ).then_inc(s_tc[0], 1)
                if b >= 1:
                    row0(b - 1)
            row0(NB - 1)
            places(1, GAT)
            dve.wait_ge(s_in["next"], 16)
            chain(V.tensor_copy(dst_f[:, :], dst_i[:, :]))
            chain(V.tensor_tensor(place[:, 0:COLS - 1], dst_f[:, 0:COLS - 1], dst_f[:, 1:], ALU.is_gt))
            chain(V.tensor_reduce(falls[:, 0:1], place[:, 0:COLS - 1], AX.X, ALU.max))
            chain(V.tensor_copy(falls[:, 1:2], dst_next[:, :]))
            chain(V.tensor_tensor(falls[:, 2:3], dst_f[:, COLS - 1:], falls[:, 1:2], ALU.is_gt))
            chain(V.tensor_tensor(falls[:, 3:4], falls[:, 0:1], falls[:, 2:3], ALU.max))
            dve.sem_inc(s_falls, 1)
            dve.wait_ge(s_falls2, 1)
            chain(V.tensor_copy(falls_i[:, :], bank[3][0:1, 0:1]))
            dve.sem_inc(s_falls3, 1)

            dve.wait_ge(s_in["w"], 64)
            dve.wait_ge(s_in["att"], 32)
            chain(V.memset(w_row[:, :], 0.0))
            chain(V.memset(pad_row[:, :], 0.0))
            V.tensor_copy(w_row[:, 0:HEADS * (HC + 1)].rearrange("p (h c) -> p h c", h=HEADS)[:, :, 0:HC],
                          w_att[:, :].rearrange("p (h c) -> p h c", h=HEADS))
            chain(V.tensor_tensor(att_tmp[:, :, :], spread(w_att[:, :].unsqueeze(1), [P, 2, D]),
                                  att[:, :, :], ALU.mult))
            chain(V.tensor_reduce(w_row[:, ROW - HEADS:].rearrange("p (s h) -> p s h", s=2),
                                  att_tmp[:, :, :].rearrange("p s (h c) -> p s h c", h=HEADS),
                                  AX.X, ALU.add))
            dve.sem_inc(s_row, 1)

            dve.wait_ge(s_paired, 1)
            for h in range(2):
                dve.wait_ge(s_sct[h], 16 * SCATTER * (COLS // TURN))
            dve.wait_ge(s_recs_load, 16)
            dve.wait_ge(s_in["bias"], 64)

            sums = acc[:, :, 0:D]

            def blocks_of(ap):
                _, values = nc.values_load_multi_w_load_instructions(
                    ap, engines=(mybir.EngineType.DVE,), min_val=0, max_val=NB - 1,
                    skip_runtime_bounds_check_because="a count of 1 to NB begun blocks, less one")
                return values

            def layer_gcn(layer):
                add = s_gadd[layer]
                V.memset(sums, 0.0).then_inc(add, 1)

                def body(q):
                    if q.live(1):
                        j = q.slot(1)
                        dve.wait_ge(s_stage[layer], q.at(1, 2, 2))
                        for t in range(GCN.step_tiles):
                            last = V.tensor_scalar(g_hot[:, j, t, :], iota[:, :], g_lw[:, j, t, 0:1],
                                                   g_lw[:, j, t, 1:2], ALU.is_equal, ALU.mult)
                        last.then_inc(s_ghot[layer], 1)
                    if q.live(2):
                        j = q.slot(2)
                        at = bass.ds(q.at(2, GCN.step_tiles), GCN.step_tiles)
                        V.tensor_copy(g_idx[:, j, :], gcn_rec[:, at, 0]).then_inc(s_stage[layer], 1)
                        V.tensor_copy(g_lw[:, j, :, :], gcn_rec[:, at, 1:3]).then_inc(s_stage[layer], 1)
                    if q.live(0):
                        blocks = blocks_of(gcn_block[0:1, bass.ds(q.at(0, GCN.part), GCN.part)])
                        dve.wait_ge(s_gpe[layer], q.at(0, GCN.part, GCN.part))
                        for g, b in enumerate(blocks):
                            dst_ap = acc[:, bass.ds(b, 1), 0:D]
                            dve.wait_ge(add, q.at(0, GCN.part, g + 1))
                            V.tensor_tensor(dst_ap, dst_ap, sum_of(g).unsqueeze(1), ALU.add
                                            ).then_inc(add, 1)
                run_steps(dve, GCN, 0, 2, body)
                dve.wait_ge(add, GCN.groups + 1)
                if layer < 2:
                    for cs in CHUNKS:
                        next_z(layer, cs)
                        dve.sem_inc(s_z[layer + 1], C)
                    chain(V.scalar_tensor_tensor(xs[:, :, :], xs[:, :, :], 1.0 if layer else 5.0, z[:, :, :],
                                                 ALU.mult, ALU.add))

            def next_z(layer, cs):
                chain(V.tensor_tensor(z[:, cs, :], acc[:, cs, 0:D],
                                      spread(inv_deg[:, cs].unsqueeze(2), [P, C, D]), ALU.mult))
                chain(V.tensor_tensor(z[:, cs, :], z[:, cs, :],
                                      spread(bias[:, layer, :].unsqueeze(1), [P, C, D]), ALU.add))
                chain(V.scalar_tensor_tensor(z[:, cs, :], z[:, cs, :], 0.01, z[:, cs, :],
                                             ALU.mult, ALU.max))

            for layer in range(3):
                layer_gcn(layer)

            def ln_stats(cs, eps):
                for b in range(cs.start, cs.stop):
                    last = V.bn_stats(stats[:, b, :], xs[:, b, :])
                chain(last)
                for b in range(cs.start, cs.stop):
                    last = V.bn_aggr(mv[:, b, :], stats[:, b, :])
                chain(last)
                chain(V.tensor_scalar(mv[:, cs, 1], mv[:, cs, 1], eps, None, ALU.add))
                dve.sem_inc(s_ln, 1)

            def ln_apply(cs, n):
                dve.wait_ge(s_ln2, n + 1)
                chain(V.reciprocal(mv[:, cs, 1], mv[:, cs, 1]))
                for b in range(cs.start, cs.stop):
                    last = V.tensor_scalar(xs[:, b, :], xs[:, b, :], mv[:, b, 0:1], mv[:, b, 1:2],
                                           ALU.subtract, ALU.mult)
                chain(last)

            for c in range(len(CHUNKS) + 1):
                if c < len(CHUNKS):
                    next_z(2, CHUNKS[c])
                    dve.sem_inc(s_third, 1)
                if c >= 1:
                    cs = CHUNKS[c - 1]
                    ln_apply(cs, c - 1)
                    chain(V.scalar_tensor_tensor(z[:, cs, :], xs[:, cs, :], 0.0, xs[:, cs, :],
                                                 ALU.not_equal, ALU.mult))
                    dve.sem_inc(s_z[3], C)
                if c < len(CHUNKS):
                    dve.wait_ge(s_added, c + 1)
                    ln_stats(CHUNKS[c], 16.0 * 1e-5)
            dve.wait_ge(s_tr[3], NB)
            V.tensor_copy(state[:, :, 0, :], acc[:, :, ROW - HEADS:ROW])
            chain(V.tensor_copy(state[:, :, 1, :], acc[:, :, ROW:]))
            first = z[:, :, 0:HEADS]
            chain(V.tensor_tensor(first, state[:, :, 0, :], state[:, :, 1, :], ALU.add))
            chain(V.scalar_tensor_tensor(state[:, :, 2, :], first, 0.2, first, ALU.mult, ALU.max))
            dve.sem_inc(sa["add"], 1)
            chain(V.tensor_tensor(xs[:, :, :], xs[:, :, :], spread(bias[:, 3, :].unsqueeze(1), [P, NB, D]),
                                  ALU.add))

            def body(q):
                m, e, h, j, k = q.slot(1), q.slot(0), q.slot(3), q.slot(-1), q.slot(-2)

                def miss(t):
                    return V.tensor_scalar(a_miss[:, h, t, :], iota_b[:, :], a_lo[:, h, t:t + 1], None,
                                           ALU.not_equal)

                if q.live(1):
                    dve.wait_ge(sa["T"], q.at(1, 1, 1))
                    V.tensor_reduce(a_max[:, m, :], wide[:, m % 2, :, :, :].rearrange("p h t e -> p h (t e)"),
                                    AX.X, ALU.max).then_inc(sa["max"], 1)
                    b, = blocks_of(gat_block[0:1, bass.ds(q.at(1), 1)])
                    top_src, a_dst, top = (state[:, bass.ds(b, 1), n, :] for n in range(3))
                    dst_top = state[:, bass.ds(b, 1), 1:3, :].rearrange("p b n h -> p b (n h)")
                if q.live(-2):
                    b2, = blocks_of(gat_block[0:1, bass.ds(q.at(-2), 1)])
                if q.live(3):
                    dve.wait_ge(sa["lo"], q.at(3, 1, 1))
                    miss(0)
                if q.live(1):
                    dve.wait_ge(sa["max"], q.at(1, 1, 1))
                    V.tensor_tensor(top_src, top_src, a_max[:, m, :].unsqueeze(1), ALU.max
                                    ).then_inc(sa["m1"], 1)
                if q.live(0):
                    dve.wait_ge(sa["node"], q.at(0, 1, 1))
                    n = bank[3][:, 0:T * 4].rearrange("p (t k) -> p t k", k=4)
                    V.tensor_tensor(a_z[:, e, :, :], n[:, :, 0:HEADS], a_rows[:, e, :, ROW - HEADS:ROW],
                                    ALU.add).then_inc(sa["e1"], 1)
                if q.live(3):
                    miss(1)
                if q.live(1):
                    dve.wait_ge(sa["m1"], q.at(1, 1, 1))
                    V.tensor_tensor(a_sum[:, m, :].unsqueeze(1), top_src, a_dst, ALU.add
                                    ).then_inc(sa["m2"], 1)
                if q.live(0):
                    dve.wait_ge(sa["e1"], q.at(0, 1, 1))
                    V.scalar_tensor_tensor(a_l[:, e, :, :], a_z[:, e, :, :], 0.2, a_z[:, e, :, :],
                                           ALU.mult, ALU.max).then_inc(sa["e2"], 1)
                if q.live(3):
                    miss(2)
                if q.live(1):
                    dve.wait_ge(sa["m2"], q.at(1, 1, 1))
                    V.scalar_tensor_tensor(a_top[:, m, :], a_sum[:, m, :], 0.2, a_sum[:, m, :],
                                           ALU.mult, ALU.max).then_inc(sa["m3"], 1)
                if q.live(0):
                    dve.wait_ge(sa["e2"], q.at(0, 1, 1))
                    V.tensor_tensor(a_l[:, e, :, :], a_l[:, e, :, :], n[:, :, HEADS:], ALU.subtract
                                    ).then_inc(sa["e3"], 1)
                if q.live(3):
                    miss(3).then_inc(sa["miss"], 1)
                if q.live(1):
                    dve.wait_ge(sa["m3"], q.at(1, 1, 1))
                    V.tensor_tensor(a_drop[:, m, :].unsqueeze(1), top, a_top[:, m, :].unsqueeze(1),
                                    ALU.subtract).then_inc(sa["m4"], 1)
                if q.live(-1):
                    dve.wait_ge(sa["p"], q.at(-1, 1, 1))
                    V.scalar_tensor_tensor(
                        a_msg[:, j, :, :].rearrange("p t (h c) -> p t h c", h=HEADS),
                        spread(a_p[:, j, :, :].unsqueeze(3), [P, T, HEADS, HC + 1]), 1.0,
                        a_rows[:, j, :, 0:ROW - HEADS].rearrange("p t (h c) -> p t h c", h=HEADS),
                        ALU.min, ALU.mult).then_inc(sa["msg"], 1)
                if q.live(1):
                    dve.wait_ge(sa["m4"], q.at(1, 1, 1))
                    V.tensor_scalar(top, a_top[:, m, :].unsqueeze(1), 1.0, None, ALU.mult
                                    ).then_inc(sa["m5"], 1)

                def add(h):
                    hs = slice(h * (HC + 1), (h + 1) * (HC + 1))
                    part = acc[:, bass.ds(b2, 1), hs]
                    return V.scalar_tensor_tensor(part, part, a_scale[:, k, h:h + 1],
                                                  bank[k % 3][:, hs].unsqueeze(1), ALU.mult, ALU.add)
                if q.live(-2):
                    dve.wait_ge(sa["scale"], q.at(-2, 1, 1))
                    dve.wait_ge(sa["pv"], q.at(-2, 1, 1))
                    dve.wait_ge(sa["add"], q.at(-2, 1, 1))
                    add(0)
                if q.live(1):
                    dve.wait_ge(sa["m5"], q.at(1, 1, 1))
                    V.tensor_scalar(a_part[:, m, 0, :].unsqueeze(1), dst_top, 1.0, None, ALU.mult
                                    ).then_inc(sa["part1"], 1)
                if q.live(-2):
                    add(1).then_inc(sa["add"], 1)
                if q.live(1):
                    dve.wait_ge(sa["part1"], q.at(1, 1, 1))
                    V.tensor_tensor(a_left[:, m, :].unsqueeze(1), dst_top, a_part[:, m, 0, :].unsqueeze(1),
                                    ALU.subtract).then_inc(sa["part2"], 1)
                if q.live(4):
                    l = q.slot(4)
                    dve.wait_ge(s_el[l], q.landed(4, 0, 2))
                    V.tensor_scalar(a_lo[:, l, :], a_edge[1][:, l, :], gat_base[:, bass.ds(q.at(4), 1)],
                                    None, ALU.subtract).then_inc(sa["lo"], 1)
                if q.live(1):
                    dve.wait_ge(sa["part2"], q.at(1, 1, 1))
                    V.tensor_scalar(a_part[:, m, 1, :], a_left[:, m, :], 1.0, None, ALU.mult
                                    ).then_inc(sa["part3"], 1)
                    dve.wait_ge(sa["part3"], q.at(1, 1, 1))
                    V.tensor_tensor(a_part[:, m, 2, :], a_left[:, m, :], a_part[:, m, 1, :], ALU.subtract
                                    ).then_inc(sa["part4"], 1)
            run_steps(dve, GAT, 2, 4, body)
            dve.wait_ge(sa["add"], GAT.steps + 1)

            den = z[:, :, 0:HEADS]
            chain(V.tensor_scalar(den, acc_v[:, :, :, HC], 1e-16, None, ALU.add))
            chain(V.reciprocal(den, den))
            dve.sem_inc(s_den, 1)
            for c in range(len(CHUNKS) + 1):
                if c < len(CHUNKS):
                    cs = CHUNKS[c]
                    dve.wait_ge(s_summed, c + 1)
                    ln_stats(cs, 1e-5)
                if c >= 1:
                    ln_apply(CHUNKS[c - 1], len(CHUNKS) + c - 1)
                    dve.sem_inc(s_fin, 1)


_INS = ["x", "src", "dst", "edge_type_4", "edge_weight", "L0_gnn_W1", "L0_gnn_b1", "L0_gnn_W2",
        "L0_gnn_b2", "L0_gnn_W3", "L0_gnn_b3", "L1_gnn_W", "L1_gnn_att_src", "L1_gnn_att_dst",
        "L1_gnn_bias"]


def kernel(**inputs):
    import numpy as _np
    import concourse.bacc as _bacc
    from concourse import mybir as _mybir
    from concourse.bass_utils import run_bass_kernel_spmd as _run

    nc = _bacc.Bacc("TRN2", target_bir_lowering=False, num_devices=1)
    arrays, args = {}, []
    for name in _INS:
        a = _np.ascontiguousarray(inputs[name])
        arrays[f"in_{name}"] = a
        args.append(nc.dram_tensor(f"in_{name}", a.shape, _mybir.dt.from_np(a.dtype),
                                   kind="ExternalInput").ap())
    out = nc.dram_tensor("out_x", (N_NODES, D), F32, kind="ExternalOutput").ap()
    gnn_kernel(nc, *args, out)
    r = _run(nc, [arrays], core_ids=[0])
    return r.results[0]["out_x"]
```
